# Optimizing a Trainium2 kernel written in Bass

```python
import numpy as np
import jax
import jax.numpy as jnp

def _softmax(x, axis=-1):
    return jax.nn.softmax(x, axis=axis)

def _gelu(x):
    return jax.nn.gelu(x, approximate=True)

def _silu(x):
    return jax.nn.silu(x)

def _sigmoid(x):
    return jax.nn.sigmoid(x)

def _layernorm(x, axis=-1, eps=1e-05):
    m = jnp.mean(x, axis=axis, keepdims=True)
    v = jnp.var(x, axis=axis, keepdims=True)
    return (x - m) / jnp.sqrt(v + eps)

def _scatter_add(tgt, idx, src, axis=0):
    return tgt.at[idx].add(src)

def _segment_sum(src, seg, n):
    return jax.ops.segment_sum(src, seg, n)
kernel_name = 'mk_conv_preact_d2_conv_nchw256_r2_41809a'

def setup_inputs(seed: int=0):
    np.random.seed(seed)
    _w = jnp.asarray

    def _rec_inputs():
        import jax
        import jax.numpy as jnp
        _gk = jax.random.key(seed)
        x = -0.0003929 + 0.9999 * jax.random.normal(jax.random.fold_in(_gk, 1), (16, 128, 32, 32), jnp.float32)
        return x
    x = _rec_inputs()

    def _L0_conv_setup():
        import jax, jax.numpy as jnp
        import numpy as np
        B, DIM, H, W = (16, 128, 32, 32)
        HEADS, DHEAD, MEM = (4, 32, 4)
        HIDDEN = HEADS * DHEAD

        def _rmsnorm(x, g):
            n = jnp.sqrt(jnp.sum(x * x, axis=1, keepdims=True))
            scale = jnp.asarray(x.shape[1], x.dtype) ** 0.5
            return x / jnp.maximum(n, 1e-12) * g[None, :, None, None] * scale
        key = jax.random.key(seed)
        ks = jax.random.split(key, 4)
        return {'x': jax.random.normal(ks[0], (B, DIM, H, W), dtype=jnp.float32), 'g1': jnp.ones((DIM,), dtype=jnp.float32), 'w_qkv': jax.random.normal(ks[1], (3 * HIDDEN, DIM), dtype=jnp.float32) * 0.02, 'mem_kv': jax.random.normal(ks[2], (2, HEADS, DHEAD, MEM), dtype=jnp.float32), 'w_out': jax.random.normal(ks[3], (DIM, HIDDEN), dtype=jnp.float32) * 0.02, 'b_out': jnp.zeros((DIM,), dtype=jnp.float32), 'g2': jnp.ones((DIM,), dtype=jnp.float32)}
    _L0_conv_all = _L0_conv_setup()
    _L0_conv_in = {k: v for k, v in _L0_conv_all.items() if k in ('g1', 'w_qkv', 'mem_kv', 'w_out', 'b_out', 'g2')}
    del _L0_conv_all

    def _L1_conv_setup():
        import jax, jax.numpy as jnp
        import numpy as np
        from jax import lax
        SPATIAL = 4
        PAD = 1
        STRIDE = 1

        def _route(x, rconv_w, rconv_b, fc_w, fc_b, num_experts):
            b, c, h, w = x.shape
            pooled = x.reshape(b, c, SPATIAL, h // SPATIAL, SPATIAL, w // SPATIAL).mean(axis=(3, 5))
            y = jnp.einsum('bcij,rc->brij', pooled, rconv_w) + rconv_b[None, :, None, None]
            y = jax.nn.relu(y).reshape(b, -1)
            y = jax.nn.relu(y @ fc_w.T + fc_b)
            y = y.reshape(b, num_experts, c)
            return jax.nn.sigmoid(y)

        def _conv_per_sample(xi, wi):
            out = lax.conv_general_dilated(xi[None], wi, window_strides=(STRIDE, STRIDE), padding=[(PAD, PAD), (PAD, PAD)], dimension_numbers=('NCHW', 'OIHW', 'NCHW'))
            return out[0]
        key = jax.random.key(seed)
        ks = jax.random.split(key, 6)
        b, c_in, c_out, kk, ne = (16, 128, 128, 3, 3)
        rc = max(c_in // 16, 16)
        x = jax.random.normal(ks[0], (b, c_in, 32, 32), dtype=jnp.float32)
        expert_weight = jax.random.normal(ks[1], (ne, c_out, c_in, kk, kk), dtype=jnp.float32) * 0.02
        rconv_w = jax.random.normal(ks[2], (rc, c_in), dtype=jnp.float32) * 0.05
        rconv_b = jax.random.normal(ks[3], (rc,), dtype=jnp.float32) * 0.05
        fc_w = jax.random.normal(ks[4], (ne * c_in, rc * SPATIAL * SPATIAL), dtype=jnp.float32) * 0.05
        fc_b = jax.random.normal(ks[5], (ne * c_in,), dtype=jnp.float32) * 0.05
        return {'x': x, 'expert_weight': expert_weight, 'rconv_w': rconv_w, 'rconv_b': rconv_b, 'fc_w': fc_w, 'fc_b': fc_b}
    _L1_conv_all = _L1_conv_setup()
    _L1_conv_in = {k: v for k, v in _L1_conv_all.items() if k in ('expert_weight', 'rconv_w', 'rconv_b', 'fc_w', 'fc_b')}
    del _L1_conv_all
    return {'x': x, 'L0_conv_g1': _L0_conv_in['g1'], 'L0_conv_w_qkv': _L0_conv_in['w_qkv'], 'L0_conv_mem_kv': _L0_conv_in['mem_kv'], 'L0_conv_w_out': _L0_conv_in['w_out'], 'L0_conv_b_out': _L0_conv_in['b_out'], 'L0_conv_g2': _L0_conv_in['g2'], 'L1_conv_expert_weight': _L1_conv_in['expert_weight'], 'L1_conv_rconv_w': _L1_conv_in['rconv_w'], 'L1_conv_rconv_b': _L1_conv_in['rconv_b'], 'L1_conv_fc_w': _L1_conv_in['fc_w'], 'L1_conv_fc_b': _L1_conv_in['fc_b']}

def reference(x, L0_conv_g1, L0_conv_w_qkv, L0_conv_mem_kv, L0_conv_w_out, L0_conv_b_out, L0_conv_g2, L1_conv_expert_weight, L1_conv_rconv_w, L1_conv_rconv_b, L1_conv_fc_w, L1_conv_fc_b):
    import jax
    import jax.numpy as jnp

    def _L0_conv_ref(x, g1, w_qkv, mem_kv, w_out, b_out, g2):
        import jax, jax.numpy as jnp
        import numpy as np
        B, DIM, H, W = (16, 128, 32, 32)
        HEADS, DHEAD, MEM = (4, 32, 4)
        HIDDEN = HEADS * DHEAD

        def _rmsnorm(x, g):
            n = jnp.sqrt(jnp.sum(x * x, axis=1, keepdims=True))
            scale = jnp.asarray(x.shape[1], x.dtype) ** 0.5
            return x / jnp.maximum(n, 1e-12) * g[None, :, None, None] * scale
        b, c, h, w = x.shape
        attn_scale = DHEAD ** (-0.5)
        xn = _rmsnorm(x, g1)
        qkv = jnp.einsum('oc,bchw->bohw', w_qkv, xn)
        qkv = qkv.reshape(b, 3, HEADS, DHEAD, h * w)
        q, k, v = (qkv[:, 0], qkv[:, 1], qkv[:, 2])
        mk = jnp.broadcast_to(mem_kv[0][None], (b, HEADS, DHEAD, MEM))
        mv = jnp.broadcast_to(mem_kv[1][None], (b, HEADS, DHEAD, MEM))
        k = jnp.concatenate([mk, k], axis=-1)
        v = jnp.concatenate([mv, v], axis=-1)
        q = jax.nn.softmax(q, axis=-2) * attn_scale
        k = jax.nn.softmax(k, axis=-1)
        context = jnp.einsum('bhdn,bhen->bhde', k, v)
        out = jnp.einsum('bhde,bhdn->bhen', context, q)
        out = out.reshape(b, HIDDEN, h, w)
        out = jnp.einsum('oc,bchw->bohw', w_out, out) + b_out[None, :, None, None]
        return _rmsnorm(out, g2)

    def _L1_conv_ref(x, expert_weight, rconv_w, rconv_b, fc_w, fc_b):
        import jax, jax.numpy as jnp
        import numpy as np
        from jax import lax
        SPATIAL = 4
        PAD = 1
        STRIDE = 1

        def _route(x, rconv_w, rconv_b, fc_w, fc_b, num_experts):
            b, c, h, w = x.shape
            pooled = x.reshape(b, c, SPATIAL, h // SPATIAL, SPATIAL, w // SPATIAL).mean(axis=(3, 5))
            y = jnp.einsum('bcij,rc->brij', pooled, rconv_w) + rconv_b[None, :, None, None]
            y = jax.nn.relu(y).reshape(b, -1)
            y = jax.nn.relu(y @ fc_w.T + fc_b)
            y = y.reshape(b, num_experts, c)
            return jax.nn.sigmoid(y)

        def _conv_per_sample(xi, wi):
            out = lax.conv_general_dilated(xi[None], wi, window_strides=(STRIDE, STRIDE), padding=[(PAD, PAD), (PAD, PAD)], dimension_numbers=('NCHW', 'OIHW', 'NCHW'))
            return out[0]
        ne = expert_weight.shape[0]
        r = _route(x, rconv_w, rconv_b, fc_w, fc_b, ne)
        w = jnp.einsum('bkc,kocij->bocij', r, expert_weight)
        out = jax.vmap(_conv_per_sample)(x, w)
        return out

    def _gn(v, G=32, eps=1e-05):
        B_, C_, H_, W_ = v.shape
        g = v.reshape(B_, G, C_ // G, H_, W_)
        m = jnp.mean(g, axis=(2, 3, 4), keepdims=True)
        s = jnp.var(g, axis=(2, 3, 4), keepdims=True)
        return ((g - m) / jnp.sqrt(s + eps)).reshape(v.shape)

    def _ln_c(v, eps=1e-06):
        m = jnp.mean(v, axis=1, keepdims=True)
        s = jnp.var(v, axis=1, keepdims=True)
        return (v - m) / jnp.sqrt(s + eps)

    def _ln_t(v, eps=1e-05):
        m = jnp.mean(v, axis=-1, keepdims=True)
        s = jnp.var(v, axis=-1, keepdims=True)
        return (v - m) / jnp.sqrt(s + eps)

    def _to_tokens(v):
        B_, C_, H_, W_ = v.shape
        return v.reshape(B_, C_, H_ * W_).transpose(0, 2, 1)

    def _from_tokens(t, like):
        B_, C_, H_, W_ = like.shape
        return t.transpose(0, 2, 1).reshape(B_, C_, H_, W_)
    x = x + _L0_conv_ref(_gn(x), L0_conv_g1, L0_conv_w_qkv, L0_conv_mem_kv, L0_conv_w_out, L0_conv_b_out, L0_conv_g2)
    x = x + _L1_conv_ref(_gn(x), L1_conv_expert_weight, L1_conv_rconv_w, L1_conv_rconv_b, L1_conv_fc_w, L1_conv_fc_b)
    return x

_drawn_inputs = setup_inputs


def setup_inputs(seed=0):
    import zlib

    import numpy as np

    out = dict(_drawn_inputs(seed))
    spreads = {'L0_conv_g1': (1.0, 0.6), 'L0_conv_b_out': (0.0, 0.1), 'L0_conv_g2': (1.0, 0.2)}
    factors = {'L0_conv_w_qkv': 8.0,
     'L0_conv_mem_kv': 8.0,
     'L0_conv_w_out': 8.0,
     'L1_conv_rconv_w': 3.292,
     'L1_conv_rconv_b': 8.0,
     'L1_conv_fc_b': 7.618}
    for name, (base, spread) in spreads.items():
        noise = np.random.default_rng([zlib.crc32(name.encode()), seed]).standard_normal(out[name].shape)
        drawn = base * np.exp(spread * noise) if base else spread * noise
        out[name] = jnp.asarray(drawn.astype(out[name].dtype))
    for name, factor in factors.items():
        out[name] = (out[name] * factor).astype(out[name].dtype)
    return out
```

```python
from contextlib import ExitStack

import concourse.bass as bass
from concourse import mybir

F32 = mybir.dt.float32
F32R = mybir.dt.float32r
ALU = mybir.AluOpType
ACT = mybir.ActivationFunctionType
AX = mybir.AxisListType


def attention_condconv_kernel(
    nc: bass.Bass,
    x: bass.AP,
    g1: bass.AP,
    w_qkv: bass.AP,
    mem_kv: bass.AP,
    w_out: bass.AP,
    b_out: bass.AP,
    g2: bass.AP,
    expert_weight: bass.AP,
    rconv_w: bass.AP,
    rconv_b: bass.AP,
    fc_w: bass.AP,
    fc_b: bass.AP,
    out: bass.AP,
):
    B, C, H, W = x.shape
    N = H * W
    NT = N // 128
    _, HEADS, DH, MEM = mem_kv.shape
    HID = HEADS * DH
    K, CO, _, KH, KW = expert_weight.shape
    TAPS = KH * KW
    RC = rconv_w.shape[0]
    SP = 4
    CELL = (H // SP) * (W // SP)
    RF = RC * SP * SP
    RCH = RF // 128
    GC = C // 32
    PH, PW = H + 2, W + 2
    HH = H // 2
    QKV = 3 * HID
    VEXT = HID + 2
    GN_EPS, NORM_MIN = 1e-5, 1e-12
    assert C == 128 and HID == 128 and CO == 128 and HH * W == 512 and RF % 128 == 0 and B % 2 == 0

    x_d = x.rearrange("b c h w -> b c (h w)")
    out_d = out.rearrange("b c h w -> b c (h w)")

    ctx = ExitStack()
    with ctx:
        def sb(name, shape, dt=F32):
            return ctx.enter_context(nc.sbuf_tensor(name, shape, dt))

        def psum(name, shape):
            return ctx.enter_context(nc.psum_tensor(name, shape, F32))

        def sem(name):
            return ctx.enter_context(nc.semaphore(name))

        ident = sb("ident", [128, 128])
        ones = sb("ones", [128, 128])
        ones_r = sb("ones_r", [128, 128], F32R)
        group_avg = sb("group_avg", [128, 128])
        head_mask = sb("head_mask", [128, 128])
        minus_half = sb("minus_half", [128, NT])
        wqkv_raw = sb("wqkv_raw", [128, 3, C])
        wqkv_t = sb("wqkv_t", [128, QKV])
        wqkv_hi = sb("wqkv_hi", [128, QKV], F32R)
        wqkv_lo = sb("wqkv_lo", [128, QKV], F32R)
        wout_raw = sb("wout_raw", [128, HID])
        wout_t = sb("wout_t", [128, C])
        bias_share = sb("bias_share", [128, C])
        bias_raw = sb("bias_raw", [128, C])
        g1_c = sb("g1_c", [128, 1])
        g2_c = sb("g2_c", [128, 1])
        mem_c = sb("mem_c", [128, 2, MEM])
        memk_max = sb("memk_max", [128, 1])
        memk_diag = sb("memk_diag", [128, 128])
        memk_t = sb("memk_t", [MEM, HID])
        memv_t = sb("memv_t", [MEM, VEXT])
        expert_raw = sb("expert_raw", [128, K, C * TAPS])
        experts = sb("experts", [128, K, TAPS * CO])
        rconv_raw = sb("rconv_raw", [RC, C])
        rconv_t = sb("rconv_t", [128, RC])
        rconv_bias = sb("rconv_bias", [128, RCH])
        fc_raw = sb("fc_raw", [128, K, RF])
        fc_t = sb("fc_t", [128, RCH, K * C])
        fc_bias = sb("fc_bias", [128, K])

        xa = [sb(f"xa{p}", [128, N]) for p in range(2)]
        stats1 = sb("stats1", [128, 2, 6])
        meanvar1 = sb("meanvar1", [128, 2])
        nmean1 = sb("nmean1", [128, 1])
        dev1 = sb("dev1", [128, 1])
        spread1 = sb("spread1", [128, 1])
        gvar1 = sb("gvar1", [128, 1])
        rstd1 = [sb(f"rstd1_{p}", [128, 1]) for p in range(2)]
        shift1 = [sb(f"shift1_{p}", [128, 1]) for p in range(2)]
        x1 = sb("x1", [128, N])
        x1_sq = sb("x1_sq", [128, N])
        x1_hi = sb("x1_hi", [128, N], F32R)
        x1_lo = sb("x1_lo", [128, N], F32R)
        ssq1 = sb("ssq1", [128, NT])
        scale1 = sb("scale1", [128, NT])
        qkv = sb("qkv", [128, NT, QKV + 2])
        k_max_part = sb("k_max_part", [128, HID])
        k_max = sb("k_max", [128, 1])
        k_diag = sb("k_diag", [128, 128], F32R)
        k_exp = sb("k_exp", [128, NT, HID])
        memk_exp = sb("memk_exp", [MEM, HID])
        q_max = sb("q_max", [128, NT * HEADS])
        q_exp = sb("q_exp", [128, NT * HEADS, DH])
        q_sum = sb("q_sum", [128, NT * HEADS])
        q_rsum = sb("q_rsum", [128, NT * HEADS])
        k_rsum = sb("k_rsum", [128, 1])
        context = sb("context", [128, HID])
        context_t = sb("context_t", [128, HID])
        q_t = [sb(f"q_t{p}", [128, N]) for p in range(2)]
        mix = [sb(f"mix{p}", [128, C]) for p in range(2)]

        xb = [sb(f"xb{p}", [128, N]) for p in range(2)]
        y_sq = sb("y_sq", [128, N])
        ssq2_sum = sb("ssq2_sum", [128, NT])
        ssq2 = sb("ssq2", [128, NT])
        scale2 = sb("scale2", [128, NT])
        y_scaled = sb("y_scaled", [128, NT, C])
        x2 = [sb(f"x2_{p}", [128, N]) for p in range(2)]
        stats2 = sb("stats2", [128, 2, 6])
        meanvar2 = sb("meanvar2", [128, 2])
        nmean2 = sb("nmean2", [128, 1])
        dev2 = sb("dev2", [128, 1])
        spread2 = sb("spread2", [128, 1])
        gvar2 = sb("gvar2", [128, 1])
        rstd2 = sb("rstd2", [128, 1])
        pooled = sb("pooled", [128, SP * SP])
        pooled_c = sb("pooled_c", [128, SP * SP])
        pooled_n = sb("pooled_n", [128, SP * SP])
        route_prod = sb("route_prod", [128, RC, SP * SP])
        route_y = sb("route_y", [128, RCH])
        route_z = sb("route_z", [128, K])
        route_zr = sb("route_zr", [128, K])
        route_e = sb("route_e", [128, K])
        route_d = sb("route_d", [128, K])
        gate = sb("gate", [128, K])
        gate_n = sb("gate_n", [128, K])
        w_first = sb("w_first", [128, TAPS * CO])
        w_second = sb("w_second", [128, TAPS * CO])
        w_full = sb("w_full", [128, TAPS * CO])
        w_hi = [sb(f"w_hi{p}", [128, TAPS, CO], F32R) for p in range(2)]
        w_lo = [sb(f"w_lo{p}", [128, TAPS, CO], F32R) for p in range(2)]
        pad_hi = [sb(f"pad_hi{p}", [128, PH, PW], F32R) for p in range(2)]
        pad_lo = [sb(f"pad_lo{p}", [128, PH, PW], F32R) for p in range(2)]

        result = [sb(f"result{p}", [128, N]) for p in range(2)]

        ps_conv = [psum(f"ps_conv{h}", [128, 512]) for h in range(2)]
        ps_qkv = [psum(f"ps_qkv{h}", [128, 512]) for h in range(2)]
        ps_y = psum("ps_y", [128, 1024])
        ps_att = psum("ps_att", [128, 512])
        ps_stat = psum("ps_stat", [128, 512])

        consts_loaded = sem("consts_loaded")
        experts_loaded = sem("experts_loaded")
        pool_zeros = sem("pool_zeros")
        pool_consts = sem("pool_consts")
        setup_pe = sem("setup_pe")
        setup_dve = sem("setup_dve")
        setup_act = sem("setup_act")
        expert_tiles = sem("expert_tiles")
        experts_ready = sem("experts_ready")
        xa_loaded = [sem(f"xa_loaded{p}") for p in range(2)]
        xb_loaded = [sem(f"xb_loaded{p}") for p in range(2)]
        stored = [sem(f"stored{p}") for p in range(2)]

        stats1_done = sem("stats1_done")
        meanvar1_done = sem("meanvar1_done")
        gmean1_ps = sem("gmean1_ps")
        nmean1_done = sem("nmean1_done")
        dev1_done = sem("dev1_done")
        spread1_done = sem("spread1_done")
        gvar1_ps = sem("gvar1_ps")
        gvar1_done = sem("gvar1_done")
        rstd1_done = sem("rstd1_done")
        shift1_done = sem("shift1_done")
        x1_started = sem("x1_started")
        stats1_read = sem("stats1_read")
        stats2_read = sem("stats2_read")
        x1_done = sem("x1_done")
        x1_sq_done = sem("x1_sq_done")
        x1_hi_done = sem("x1_hi_done")
        x1_lo_done = sem("x1_lo_done")
        ssq1_ps = sem("ssq1_ps")
        ssq1_done = sem("ssq1_done")
        scale1_done = sem("scale1_done")
        qkv_ps = sem("qkv_ps")
        qkv_done = sem("qkv_done")
        k_part_done = sem("k_part_done")
        k_part_ps = sem("k_part_ps")
        k_max_done = sem("k_max_done")
        k_diag_done = sem("k_diag_done")
        k_shift_ps = sem("k_shift_ps")
        k_sub_done = sem("k_sub_done")
        memk_sub_done = sem("memk_sub_done")
        k_exp_done = sem("k_exp_done")
        memk_exp_done = sem("memk_exp_done")
        q_max_done = sem("q_max_done")
        q_sub_done = sem("q_sub_done")
        q_exp_done = sem("q_exp_done")
        q_sum_done = sem("q_sum_done")
        q_rsum_done = sem("q_rsum_done")
        q_norm_done = sem("q_norm_done")
        context_ps = sem("context_ps")
        k_rsum_done = sem("k_rsum_done")
        context_done = sem("context_done")
        context_t_ps = sem("context_t_ps")
        context_t_done = sem("context_t_done")
        mix_ps = sem("mix_ps")
        mix_done = sem("mix_done")
        q_t_ps = sem("q_t_ps")
        q_t_done = sem("q_t_done")

        y_ps = sem("y_ps")
        y_sq_done = sem("y_sq_done")
        ssq2_sum_done = sem("ssq2_sum_done")
        ssq2_done = sem("ssq2_done")
        scale2_done = sem("scale2_done")
        y_scaled_done = sem("y_scaled_done")
        y_t_ps = sem("y_t_ps")
        x2_done = sem("x2_done")
        stats2_done = sem("stats2_done")
        meanvar2_done = sem("meanvar2_done")
        pooled_done = sem("pooled_done")
        gmean2_ps = sem("gmean2_ps")
        nmean2_done = sem("nmean2_done")
        dev2_done = sem("dev2_done")
        spread2_done = sem("spread2_done")
        gvar2_ps = sem("gvar2_ps")
        gvar2_done = sem("gvar2_done")
        rstd2_done = sem("rstd2_done")
        pooled_c_done = sem("pooled_c_done")
        pooled_n_done = sem("pooled_n_done")
        route_prod_done = sem("route_prod_done")
        route_y_ps = sem("route_y_ps")
        route_y_done = sem("route_y_done")
        route_z_ps = sem("route_z_ps")
        route_z_done = sem("route_z_done")
        route_zr_done = sem("route_zr_done")
        route_e_done = sem("route_e_done")
        route_d_done = sem("route_d_done")
        gate_done = sem("gate_done")
        gate_n_done = sem("gate_n_done")
        w_first_done = sem("w_first_done")
        w_second_done = sem("w_second_done")
        w_full_done = sem("w_full_done")
        w_hi_done = sem("w_hi_done")
        w_lo_done = sem("w_lo_done")
        pad_hi_done = sem("pad_hi_done")
        pad_lo_done = sem("pad_lo_done")
        conv_ps = sem("conv_ps")
        result_done = sem("result_done")

        def tile(t):
            return slice(128 * t, 128 * t + 128)

        def half(h):
            return slice(512 * h, 512 * h + 512)

        def interior(pad, lo=0, hi=H):
            return pad[:, 1 + lo:1 + hi, 1:1 + W]

        def image(flat, lo=0, hi=H):
            return flat[:, lo * W:hi * W].rearrange("p (h w) -> p h w", w=W)

        def past(b, n):
            return not isinstance(b, int) or b >= n

        def slot_count(b, p):
            return 8 * (b - p) + 16

        FIRST, LAST = 4, B - 2

        def run_steps(eng, step):
            for t in range(FIRST):
                step(t, t % 2, True, t >= 1, t >= 2)
            with eng.Fori(FIRST, LAST - 1, 2) as i:
                step(i, 0, True, True, True)
                step(i + 1, 1, True, True, True)
            for t in range(LAST, B + 2):
                step(t, t % 2, t < B, t <= B, True)

        block = ctx.enter_context(nc.Block())

        @block.sync
        def _(sp):
            def load_xa(b, p):
                if past(b, 2):
                    sp.wait_ge(x1_done, b - 1)
                    sp.wait_ge(x1_hi_done, b - 1)
                    sp.wait_ge(x1_sq_done, b - 1)
                sp.dma_start(xa[p][:, :], x_d[b]).then_inc(xa_loaded[p], 16)

            def load_xb(b, p):
                if past(b, 2):
                    sp.wait_ge(x2_done, b - 1)
                sp.dma_start(xb[p][:, :], x_d[b]).then_inc(xb_loaded[p], 16)

            def store(b, p):
                sp.wait_ge(result_done, 2 * (b + 1))
                sp.dma_start(out_d[b], result[p][:, :]).then_inc(stored[p], 16)

            load_xa(0, 0)
            sp.dma_start(wqkv_raw[:, :, :], w_qkv.rearrange("(s o) c -> o s c", s=3)).then_inc(consts_loaded, 16)
            sp.dma_start(g1_c[:, :], g1.rearrange("(c a) -> c a", a=1)).then_inc(consts_loaded, 16)
            sp.dma_start(mem_c[:, :, :], mem_kv.rearrange("s h d m -> (h d) s m")).then_inc(consts_loaded, 16)
            sp.dma_start(wout_raw[:, :], w_out).then_inc(consts_loaded, 16)
            sp.dma_start(g2_c[:, :], g2.rearrange("(c a) -> c a", a=1)).then_inc(consts_loaded, 16)
            sp.dma_start(bias_raw[:, :], b_out.rearrange("(a c) -> a c", a=1).to_broadcast((128, C))).then_inc(consts_loaded, 16)
            sp.dma_start(rconv_raw[:, :], rconv_w).then_inc(consts_loaded, 16)
            for r in range(RC):
                rows = SP * SP
                at = (r % (RC // RCH)) * rows
                ch = r // (RC // RCH)
                sp.dma_start(rconv_bias[at:at + rows, ch:ch + 1],
                             rconv_b[r:r + 1].rearrange("(c a) -> c a", a=1).to_broadcast((rows, 1))).then_inc(consts_loaded, 16)
            sp.dma_start(fc_raw[:, :, :], fc_w.rearrange("(k c) j -> c k j", k=K)).then_inc(consts_loaded, 16)
            sp.dma_start(fc_bias[:, :], fc_b.rearrange("(k c) -> c k", k=K), allow_slow_non_contiguous=True).then_inc(consts_loaded, 16)
            load_xa(1, 1)
            sp.dma_start(expert_raw[:, :, :], expert_weight.rearrange("k o c i j -> o k (c i j)")).then_inc(experts_loaded, 16)

            def step(t, p, a, b, c):
                if b:
                    load_xb(t - 1, 1 - p)
                if a and not (isinstance(t, int) and t + 2 >= B):
                    load_xa(t + 2, p)
                if c:
                    store(t - 2, p)

            run_steps(sp, step)
            for p in range(2):
                sp.wait_ge(stored[p], 16 * (B // 2))

        CONSTS = 16 * (9 + RC)

        @block.gpsimd
        def _(pool):
            nc.gpsimd.memset(ident[:, :], 0.0)
            nc.gpsimd.memset(group_avg[:, :], 1.0 / GC)
            nc.gpsimd.memset(head_mask[:, :], float(DH) ** -0.5)
            nc.gpsimd.memset(memv_t[:, :], 1.0)
            for p in range(2):
                nc.gpsimd.memset(pad_hi[p][:, :, :].bitcast(F32), 0.0)
                nc.gpsimd.memset(pad_lo[p][:, :, :].bitcast(F32), 0.0)
            nc.gpsimd.memset(qkv[:, :, QKV:QKV + 2], 1.0)
            nc.gpsimd.memset(ones[:, :], 1.0).then_inc(pool_zeros, 1)
            pool.wait_ge(pool_zeros, 1)
            nc.gpsimd.affine_select(out=ident[:, :], in_=ident[:, :], compare_op=ALU.not_equal, fill=1.0,
                                    base=0, pattern=[[-1, 128]], channel_multiplier=1)
            for mask, size in ((group_avg, GC), (head_mask, DH)):
                blocks = mask[:, :].rearrange("p (g j) -> p g j", j=size)
                nc.gpsimd.affine_select(out=blocks, in_=blocks, compare_op=ALU.is_ge, fill=0.0, base=0,
                                        pattern=[[-size, 128 // size], [0, size]], channel_multiplier=1)
            nc.gpsimd.memset(minus_half[:, :], -0.5).then_inc(pool_zeros, 1)
            pool.wait_ge(pool_zeros, 2)
            for mask, size in ((group_avg, GC), (head_mask, DH)):
                blocks = mask[:, :].rearrange("p (g j) -> p g j", j=size)
                last = nc.gpsimd.affine_select(out=blocks, in_=blocks, compare_op=ALU.is_ge, fill=0.0, base=size - 1,
                                               pattern=[[size, 128 // size], [0, size]], channel_multiplier=-1)
            last.then_inc(pool_consts, 1)

            def gn1(b, p):
                pool.wait_ge(gvar1_done, b + 1)
                if past(b, 2):
                    pool.wait_ge(x1_done, b - 1)
                    pool.wait_ge(x1_hi_done, b - 1)
                nc.gpsimd.tensor_tensor(rstd1[p][:, :], gvar1[:, :], minus_half[:, 0:1], ALU.pow).then_inc(rstd1_done, 1)
                pool.wait_ge(rstd1_done, b + 1)
                nc.gpsimd.tensor_tensor(shift1[p][:, :], nmean1[:, :], rstd1[p][:, :], ALU.mult).then_inc(shift1_done, 1)

            def normalise1(b, p):
                pool.wait_ge(xa_loaded[p], slot_count(b, p))
                if past(b, 1):
                    pool.wait_ge(x1_lo_done, b)
                pool.wait_ge(shift1_done, b + 1).then_inc(x1_started, 1)
                nc.gpsimd.tensor_scalar(x1[:, :], xa[p][:, :], rstd1[p][:, :], shift1[p][:, :], ALU.mult, ALU.add).then_inc(x1_done, 1)
                pool.wait_ge(x1_done, b + 1)
                pool.wait_ge(x1_hi_done, b + 1)
                if past(b, 1):
                    pool.wait_ge(qkv_ps, NT * b)
                nc.gpsimd.tensor_tensor(x1_lo[:, :], x1[:, :], x1_hi[:, :].bitcast(F32), ALU.subtract).then_inc(x1_lo_done, 1)

            def rms1(b, p):
                pool.wait_ge(ssq1_done, b + 1)
                if past(b, 1):
                    pool.wait_ge(qkv_done, NT * b)
                nc.gpsimd.tensor_tensor(scale1[:, :], ssq1[:, :], minus_half[:, :], ALU.pow).then_inc(scale1_done, 1)

            def q_normalise(b, p):
                pool.wait_ge(q_rsum_done, b + 1)
                nc.gpsimd.tensor_tensor(q_exp[:, :, :], q_exp[:, :, :],
                                        q_rsum[:, :].unsqueeze(2).to_broadcast((128, NT * HEADS, DH)),
                                        ALU.mult).then_inc(q_norm_done, 1)

            def rms2(b, p):
                pool.wait_ge(ssq2_done, b + 1)
                if past(b, 1):
                    pool.wait_ge(y_scaled_done, b)
                nc.gpsimd.tensor_tensor(scale2[:, :], ssq2[:, :], minus_half[:, :], ALU.pow).then_inc(scale2_done, 1)

            def gn2(b, p):
                pool.wait_ge(gvar2_done, b + 1)
                if past(b, 1):
                    pool.wait_ge(gate_n_done, b)
                nc.gpsimd.tensor_tensor(rstd2[:, :], gvar2[:, :], minus_half[:, 0:1], ALU.pow).then_inc(rstd2_done, 1)

            def pooled_products(b, p):
                pool.wait_ge(pooled_c_done, b + 1)
                pool.wait_ge(rstd2_done, b + 1)
                nc.gpsimd.tensor_tensor(pooled_n[:, :], pooled_c[:, :], rstd2[:, :].to_broadcast((128, SP * SP)), ALU.mult).then_inc(pooled_n_done, 1)
                pool.wait_ge(pooled_n_done, b + 1)
                if past(b, 1):
                    pool.wait_ge(route_y_ps, b)
                nc.gpsimd.tensor_tensor(route_prod[:, :, :],
                                        rconv_t[:, :].unsqueeze(2).to_broadcast((128, RC, SP * SP)),
                                        pooled_n[:, :].unsqueeze(1).to_broadcast((128, RC, SP * SP)),
                                        ALU.mult).then_inc(route_prod_done, 1)

            def filters_low(b, p):
                pool.wait_ge(w_full_done, b + 1)
                pool.wait_ge(w_hi_done, b + 1)
                if past(b, 2):
                    pool.wait_ge(conv_ps, 2 * (b - 1))
                nc.gpsimd.tensor_tensor(w_lo[p][:, :, :].rearrange("p t o -> p (t o)"), w_full[:, :],
                                        w_hi[p][:, :, :].bitcast(F32).rearrange("p t o -> p (t o)"),
                                        ALU.subtract).then_inc(w_lo_done, 1)

            pool.wait_ge(setup_dve, 1)
            gn1(0, 0)

            def step(t, p, a, b, c):
                if a:
                    normalise1(t, p)
                if b:
                    rms2(t - 1, 1 - p)
                if a:
                    rms1(t, p)
                if b:
                    gn2(t - 1, 1 - p)
                    pooled_products(t - 1, 1 - p)
                if a:
                    q_normalise(t, p)
                if b:
                    filters_low(t - 1, 1 - p)
                if a and not (isinstance(t, int) and t + 1 >= B):
                    gn1(t + 1, 1 - p)

            run_steps(pool, step)

        @block.scalar
        def _(act):
            act.wait_ge(pool_zeros, 1)
            nc.scalar.activation(ones_r[:, :], ones[:, :], ACT.Copy).then_inc(setup_act, 1)
            act.wait_ge(setup_dve, 1)
            nc.scalar.activation(wqkv_hi[:, :], wqkv_t[:, :], ACT.Copy).then_inc(setup_act, 1)

            def square_and_high1(b, p):
                act.wait_ge(shift1_done, b + 1)
                act.wait_ge(xa_loaded[p], slot_count(b, p))
                if past(b, 1):
                    act.wait_ge(ssq1_ps, b)
                nc.scalar.activation(x1_sq[:, :], xa[p][:, :], ACT.Square, bias=shift1[p][:, :], scale=rstd1[p][:, :]).then_inc(x1_sq_done, 1)
                if past(b, 1):
                    act.wait_ge(qkv_ps, NT * b)
                    act.wait_ge(x1_lo_done, b)
                nc.scalar.activation(x1_hi[:, :], xa[p][:, :], ACT.Identity, bias=shift1[p][:, :], scale=rstd1[p][:, :]).then_inc(x1_hi_done, 1)

            def qkv_evacuate(b, p):
                act.wait_ge(scale1_done, b + 1)
                if past(b, 1):
                    act.wait_ge(k_sub_done, b)
                    act.wait_ge(q_sub_done, b)
                    act.wait_ge(context_ps, b)
                for t in range(NT):
                    act.wait_ge(qkv_ps, NT * b + t + 1)
                    nc.scalar.activation(qkv[:, t, 0:QKV], ps_qkv[t % 2][:, 0:QKV], ACT.Copy, scale=scale1[:, t:t + 1]).then_inc(qkv_done, 1)

            def k_exponent(b, p):
                act.wait_ge(memk_sub_done, b + 1)
                nc.scalar.activation(memk_exp[:, :], memk_exp[:, :], ACT.Exp).then_inc(memk_exp_done, 1)
                act.wait_ge(k_sub_done, b + 1)
                nc.scalar.activation(k_exp[:, :, :], k_exp[:, :, :], ACT.Exp).then_inc(k_exp_done, 1)

            def q_exponent(b, p):
                act.wait_ge(q_sub_done, b + 1)
                nc.scalar.activation(q_exp[:, :, :], q_exp[:, :, :], ACT.Exp).then_inc(q_exp_done, 1)

            def context_evacuate(b, p):
                act.wait_ge(context_t_ps, b + 1)
                if past(b, 1):
                    act.wait_ge(mix_ps, b)
                nc.scalar.activation(context_t[:, :], ps_att[:, 0:HID], ACT.Copy).then_inc(context_t_done, 1)

            def q_evacuate(b, p):
                if past(b, 2):
                    act.wait_ge(y_ps, b - 1)
                for h in range(2):
                    act.wait_ge(q_t_ps, 2 * b + h + 1)
                    nc.scalar.activation(q_t[p][:, half(h)], ps_qkv[h][:, :], ACT.Copy).then_inc(q_t_done, 1)

            def square2(b, p):
                act.wait_ge(y_ps, b + 1)
                if past(b, 1):
                    act.wait_ge(ssq2_sum_done, b)
                nc.scalar.activation(y_sq[:, :], ps_y[:, :], ACT.Square).then_inc(y_sq_done, 1)

            def image_high(b, p):
                act.wait_ge(nmean2_done, b + 1)
                if past(b, 2):
                    act.wait_ge(conv_ps, 2 * (b - 1))
                nc.scalar.activation(interior(pad_hi[p]), image(x2[p]), ACT.Identity, bias=nmean2[:, :]).then_inc(pad_hi_done, 1)

            def gate_exponent(b, p):
                act.wait_ge(route_zr_done, b + 1)
                nc.scalar.activation(route_e[:, :], route_zr[:, :], ACT.Exp, scale=-1.0).then_inc(route_e_done, 1)

            def filters_first(b, p):
                act.wait_ge(gate_n_done, b + 1)
                if past(b, 1):
                    act.wait_ge(w_second_done, b)
                nc.scalar.activation(w_first[:, :], experts[:, 0, :], ACT.Copy, scale=gate_n[:, 0:1]).then_inc(w_first_done, 1)

            def filters_high(b, p):
                act.wait_ge(w_full_done, b + 1)
                if past(b, 2):
                    act.wait_ge(conv_ps, 2 * (b - 1))
                nc.scalar.activation(w_hi[p][:, :, :].rearrange("p t o -> p (t o)"), w_full[:, :], ACT.Copy).then_inc(w_hi_done, 1)

            def experts_evacuate():
                n = 0
                for k in range(K):
                    for first in range(0, TAPS, 4):
                        taps = min(4, TAPS - first)
                        act.wait_ge(expert_tiles, n + 1)
                        last = nc.scalar.activation(experts[:, k, first * CO:(first + taps) * CO],
                                                    ps_conv[n % 2][:, 0:taps * CO], ACT.Copy).then_inc(experts_ready, 1)
                        n += 1

            def step(t, p, a, b, c):
                if a:
                    square_and_high1(t, p)
                if b:
                    square2(t - 1, 1 - p)
                if a:
                    qkv_evacuate(t, p)
                if b:
                    image_high(t - 1, 1 - p)
                if a:
                    k_exponent(t, p)
                    q_exponent(t, p)
                if b:
                    gate_exponent(t - 1, 1 - p)
                    filters_first(t - 1, 1 - p)
                if a:
                    context_evacuate(t, p)
                if b:
                    filters_high(t - 1, 1 - p)
                if a:
                    q_evacuate(t, p)
                if isinstance(t, int) and t == 0:
                    experts_evacuate()

            run_steps(act, step)

        EXPERT_FILLS = K * -(-TAPS // 4)

        @block.vector
        def _(dve):
            v = nc.vector
            dve.wait_ge(consts_loaded, CONSTS)
            dve.wait_ge(setup_pe, 1)
            v.tensor_scalar(wqkv_t[:, :], ps_y[:, 0:QKV], g1_c[:, :], None, ALU.mult)
            v.tensor_copy(rconv_t[:, :], ps_y[:, 512:512 + RC]).then_inc(setup_dve, 1)
            dve.wait_ge(setup_act, 2)
            v.tensor_tensor(wqkv_lo[:, :], wqkv_t[:, :], wqkv_hi[:, :].bitcast(F32), ALU.subtract).then_inc(setup_dve, 1)

            dve.wait_ge(setup_pe, 2)
            v.tensor_copy(wout_t[:, :], ps_att[:, 0:C])
            v.tensor_copy(memk_t[:, :], ps_att[0:MEM, 128:256])
            v.tensor_copy(memv_t[:, 0:HID], ps_att[0:MEM, 256:384])
            v.tensor_scalar(bias_share[:, :], bias_raw[:, :], 1.0 / HEADS, None, ALU.mult)
            v.tensor_reduce(memk_max[:, :], mem_c[:, 0, :], AX.X, ALU.max).then_inc(setup_dve, 1)
            dve.wait_ge(setup_dve, 3)
            v.tensor_scalar(memk_diag[:, :], ident[:, :], memk_max[:, :], None, ALU.mult).then_inc(setup_dve, 1)
            for ch in range(RCH):
                dve.wait_ge(setup_pe, 3 + ch)
                v.tensor_copy(fc_t[:, ch, :], ps_y[:, 512 * ch:512 * ch + K * C]).then_inc(setup_dve, 1)
            dve.wait_ge(setup_dve, 4 + RCH)

            def gn1_stats(b, p):
                dve.wait_ge(xa_loaded[p], slot_count(b, p))
                if past(b, 1):
                    dve.wait_ge(meanvar1_done, b)
                for h in range(2):
                    last = v.bn_stats(stats1[:, h, :], xa[p][:, half(h)])
                last.then_inc(stats1_done, 1)
                if past(b, 1):
                    dve.wait_ge(gmean1_ps, b)
                    dve.wait_ge(spread1_done, b)
                dve.wait_ge(stats1_done, b + 1).then_inc(stats1_read, 1)
                v.bn_aggr(meanvar1[:, :], stats1[:, :, :].rearrange("p h s -> p (h s)")).then_inc(meanvar1_done, 1)

            def gn1_spread(b, p):
                dve.wait_ge(gmean1_ps, b + 1)
                if past(b, 1):
                    dve.wait_ge(shift1_done, b)
                v.tensor_scalar(nmean1[:, :], ps_stat[:, 0:1], -1.0, None, ALU.mult).then_inc(nmean1_done, 1)
                dve.wait_ge(nmean1_done, b + 1)
                v.tensor_tensor(dev1[:, :], meanvar1[:, 0:1], nmean1[:, :], ALU.add).then_inc(dev1_done, 1)
                dve.wait_ge(dev1_done, b + 1)
                if past(b, 1):
                    dve.wait_ge(gvar1_ps, b)
                v.scalar_tensor_tensor(spread1[:, :], dev1[:, :], dev1[:, :], meanvar1[:, 1:2], ALU.mult, ALU.add).then_inc(spread1_done, 1)

            def gn1_var(b, p):
                dve.wait_ge(gvar1_ps, b + 1)
                if past(b, 1):
                    dve.wait_ge(rstd1_done, b)
                v.tensor_scalar(gvar1[:, :], ps_stat[:, 0:1], GN_EPS, None, ALU.add).then_inc(gvar1_done, 1)

            def rms1(b, p):
                dve.wait_ge(ssq1_ps, b + 1)
                if past(b, 1):
                    dve.wait_ge(scale1_done, b)
                v.tensor_scalar(ssq1[:, :], ps_stat[:, 0:NT], 1.0 / C, NORM_MIN ** 2 / C, ALU.mult, ALU.max).then_inc(ssq1_done, 1)

            def k_partial_max(b, p):
                dve.wait_ge(qkv_done, NT * (b + 1))
                if past(b, 1):
                    dve.wait_ge(k_part_ps, b)
                v.tensor_reduce(k_max_part[:, :], qkv[:, :, HID:2 * HID].rearrange("p t c -> p c t"), AX.X, ALU.max).then_inc(k_part_done, 1)

            def k_maximum(b, p):
                dve.wait_ge(k_part_ps, b + 1)
                if past(b, 1):
                    dve.wait_ge(k_diag_done, b)
                v.tensor_reduce(k_max[:, :], ps_att[:, 0:128], AX.X, ALU.max).then_inc(k_max_done, 1)
                dve.wait_ge(k_max_done, b + 1)
                if past(b, 1):
                    dve.wait_ge(k_shift_ps, b)
                v.scalar_tensor_tensor(k_diag[:, :], ident[:, :], k_max[:, :], memk_diag[:, :], ALU.mult, ALU.max).then_inc(k_diag_done, 1)

            def k_subtract(b, p):
                dve.wait_ge(k_shift_ps, b + 1)
                if past(b, 1):
                    dve.wait_ge(context_ps, b)
                v.tensor_tensor(memk_exp[:, :], memk_t[:, :], ps_att[0:MEM, 0:HID], ALU.subtract).then_inc(memk_sub_done, 1)
                v.tensor_tensor(k_exp[:, :, :], qkv[:, :, HID:2 * HID],
                                ps_att[:, 0:HID].unsqueeze(1).to_broadcast((128, NT, HID)), ALU.subtract).then_inc(k_sub_done, 1)

            def q_subtract(b, p):
                q = qkv[:, :, 0:HID].rearrange("p t (h d) -> p t h d", h=HEADS)
                if past(b, 1):
                    dve.wait_ge(q_sub_done, b)
                v.tensor_reduce(q_max[:, :].rearrange("p (t h) -> p t h", h=HEADS), q, AX.X, ALU.max).then_inc(q_max_done, 1)
                dve.wait_ge(q_max_done, b + 1)
                if past(b, 1):
                    dve.wait_ge(q_t_ps, 2 * b)
                v.tensor_tensor(q_exp[:, :, :].rearrange("p (t h) d -> p t h d", h=HEADS), q,
                                q_max[:, :].rearrange("p (t h) -> p t h", h=HEADS).unsqueeze(3).to_broadcast((128, NT, HEADS, DH)),
                                ALU.subtract).then_inc(q_sub_done, 1)

            def q_sums(b, p):
                dve.wait_ge(q_exp_done, b + 1)
                if past(b, 1):
                    dve.wait_ge(q_rsum_done, b)
                v.tensor_reduce(q_sum[:, :], q_exp[:, :, :], AX.X, ALU.add).then_inc(q_sum_done, 1)
                dve.wait_ge(q_sum_done, b + 1)
                if past(b, 1):
                    dve.wait_ge(q_norm_done, b)
                v.reciprocal(q_rsum[:, :], q_sum[:, :]).then_inc(q_rsum_done, 1)

            def context_scale(b, p):
                dve.wait_ge(context_ps, b + 1)
                if past(b, 1):
                    dve.wait_ge(context_done, b)
                v.reciprocal(k_rsum[:, :], ps_att[:, HID:HID + 1]).then_inc(k_rsum_done, 1)
                dve.wait_ge(k_rsum_done, b + 1)
                if past(b, 1):
                    dve.wait_ge(context_t_ps, b)
                v.scalar_tensor_tensor(context[:, :], ps_att[:, 0:HID], k_rsum[:, :], head_mask[:, :], ALU.mult, ALU.mult).then_inc(context_done, 1)

            def mix_evacuate(b, p):
                dve.wait_ge(mix_ps, b + 1)
                if past(b, 2):
                    dve.wait_ge(y_ps, b - 1)
                v.tensor_tensor(mix[p][:, :], ps_att[:, 0:C], bias_share[:, :], ALU.add).then_inc(mix_done, 1)

            def rms2_sum(b, p):
                dve.wait_ge(y_sq_done, b + 1)
                if past(b, 1):
                    dve.wait_ge(ssq2_done, b)
                v.tensor_reduce(ssq2_sum[:, :], y_sq[:, :].rearrange("p (t c) -> p t c", c=C), AX.X, ALU.add).then_inc(ssq2_sum_done, 1)
                dve.wait_ge(ssq2_sum_done, b + 1)
                if past(b, 1):
                    dve.wait_ge(scale2_done, b)
                v.tensor_scalar(ssq2[:, :], ssq2_sum[:, :], 1.0 / C, NORM_MIN ** 2 / C, ALU.mult, ALU.max).then_inc(ssq2_done, 1)

            def y_scale(b, p):
                dve.wait_ge(scale2_done, b + 1)
                if past(b, 1):
                    dve.wait_ge(y_t_ps, b)
                v.tensor_tensor(y_scaled[:, :, :], ps_y[:, :].rearrange("p (t c) -> p t c", c=C),
                                scale2[:, :].unsqueeze(2).to_broadcast((128, NT, C)), ALU.mult).then_inc(y_scaled_done, 1)

            def residual1(b, p):
                dve.wait_ge(y_t_ps, b + 1)
                dve.wait_ge(xb_loaded[p], slot_count(b, p))
                if past(b, 2):
                    dve.wait_ge(result_done, 2 * (b - 1))
                v.scalar_tensor_tensor(x2[p][:, :], ps_y[:, :], g2_c[:, :], xb[p][:, :], ALU.mult, ALU.add).then_inc(x2_done, 1)

            def gn2_stats(b, p):
                dve.wait_ge(x2_done, b + 1)
                if past(b, 1):
                    dve.wait_ge(meanvar2_done, b)
                for h in range(2):
                    last = v.bn_stats(stats2[:, h, :], x2[p][:, half(h)])
                last.then_inc(stats2_done, 1)
                if past(b, 1):
                    dve.wait_ge(gmean2_ps, b)
                    dve.wait_ge(spread2_done, b)
                dve.wait_ge(stats2_done, b + 1).then_inc(stats2_read, 1)
                v.bn_aggr(meanvar2[:, :], stats2[:, :, :].rearrange("p h s -> p (h s)")).then_inc(meanvar2_done, 1)
                if past(b, 1):
                    dve.wait_ge(pooled_c_done, b)
                v.tensor_reduce(pooled[:, :].rearrange("p (i j) -> p i j", j=SP),
                                x2[p][:, :].rearrange("p (i a j b) -> p i j a b", i=SP, j=SP, b=W // SP), AX.XY, ALU.add).then_inc(pooled_done, 1)

            def gn2_spread(b, p):
                dve.wait_ge(gmean2_ps, b + 1)
                if past(b, 1):
                    dve.wait_ge(pad_hi_done, b)
                    dve.wait_ge(pad_lo_done, b)
                v.tensor_scalar(nmean2[:, :], ps_stat[:, 0:1], -1.0, None, ALU.mult).then_inc(nmean2_done, 1)
                dve.wait_ge(nmean2_done, b + 1)
                if past(b, 1):
                    dve.wait_ge(pooled_n_done, b)
                v.tensor_scalar(pooled_c[:, :], pooled[:, :], 1.0 / CELL, nmean2[:, :], ALU.mult, ALU.add).then_inc(pooled_c_done, 1)
                v.tensor_tensor(dev2[:, :], meanvar2[:, 0:1], nmean2[:, :], ALU.add).then_inc(dev2_done, 1)
                dve.wait_ge(dev2_done, b + 1)
                if past(b, 1):
                    dve.wait_ge(gvar2_ps, b)
                v.scalar_tensor_tensor(spread2[:, :], dev2[:, :], dev2[:, :], meanvar2[:, 1:2], ALU.mult, ALU.add).then_inc(spread2_done, 1)

            def gn2_var(b, p):
                dve.wait_ge(gvar2_ps, b + 1)
                if past(b, 1):
                    dve.wait_ge(rstd2_done, b)
                v.tensor_scalar(gvar2[:, :], ps_stat[:, 0:1], GN_EPS, None, ALU.add).then_inc(gvar2_done, 1)

            def image_low(b, p):
                dve.wait_ge(nmean2_done, b + 1)
                dve.wait_ge(pad_hi_done, b + 1)
                if past(b, 2):
                    dve.wait_ge(conv_ps, 2 * (b - 1))
                v.scalar_tensor_tensor(interior(pad_lo[p]), image(x2[p]), nmean2[:, :],
                                       interior(pad_hi[p]).bitcast(F32), ALU.add, ALU.subtract).then_inc(pad_lo_done, 1)

            def route_first(b, p):
                dve.wait_ge(route_y_ps, b + 1)
                if past(b, 1):
                    dve.wait_ge(route_z_ps, b)
                for ch in range(RCH):
                    last = v.tensor_scalar(route_y[:, ch:ch + 1], ps_stat[:, ch:ch + 1], rconv_bias[:, ch:ch + 1], 0.0, ALU.add, ALU.max)
                last.then_inc(route_y_done, 1)

            def route_second(b, p):
                dve.wait_ge(route_z_ps, b + 1)
                if past(b, 1):
                    dve.wait_ge(route_zr_done, b)
                v.tensor_tensor(route_z[:, :], ps_stat[:, 0:K], fc_bias[:, :], ALU.add).then_inc(route_z_done, 1)
                dve.wait_ge(route_z_done, b + 1)
                if past(b, 1):
                    dve.wait_ge(route_e_done, b)
                v.tensor_scalar(route_zr[:, :], route_z[:, :], 0.0, None, ALU.max).then_inc(route_zr_done, 1)

            def gates(b, p):
                dve.wait_ge(route_e_done, b + 1)
                if past(b, 1):
                    dve.wait_ge(gate_done, b)
                v.tensor_scalar(route_d[:, :], route_e[:, :], 1.0, None, ALU.add).then_inc(route_d_done, 1)
                dve.wait_ge(route_d_done, b + 1)
                if past(b, 1):
                    dve.wait_ge(gate_n_done, b)
                v.reciprocal(gate[:, :], route_d[:, :]).then_inc(gate_done, 1)
                dve.wait_ge(gate_done, b + 1)
                dve.wait_ge(rstd2_done, b + 1)
                if past(b, 1):
                    dve.wait_ge(w_full_done, b)
                    dve.wait_ge(w_first_done, b)
                v.tensor_scalar(gate_n[:, :], gate[:, :], rstd2[:, :], None, ALU.mult).then_inc(gate_n_done, 1)

            def filters(b, p):
                dve.wait_ge(gate_n_done, b + 1)
                dve.wait_ge(w_first_done, b + 1)
                if past(b, 1):
                    dve.wait_ge(w_full_done, b)
                v.scalar_tensor_tensor(w_second[:, :], experts[:, 1, :], gate_n[:, 1:2], w_first[:, :], ALU.mult, ALU.add).then_inc(w_second_done, 1)
                dve.wait_ge(w_second_done, b + 1)
                if past(b, 1):
                    dve.wait_ge(w_hi_done, b)
                    dve.wait_ge(w_lo_done, b)
                v.scalar_tensor_tensor(w_full[:, :], experts[:, 2, :], gate_n[:, 2:3], w_second[:, :], ALU.mult, ALU.add).then_inc(w_full_done, 1)

            def residual2(b, p, h):
                dve.wait_ge(conv_ps, 2 * b + h + 1)
                if past(b, 2):
                    dve.wait_ge(stored[p], slot_count(b - 2, p))
                v.tensor_tensor(result[p][:, half(h)], ps_conv[h][:, :], x2[p][:, half(h)], ALU.add).then_inc(result_done, 1)

            def step(t, p, a, b, c):
                if b:
                    rms2_sum(t - 1, 1 - p)
                if a:
                    rms1(t, p)
                if b:
                    y_scale(t - 1, 1 - p)
                    residual1(t - 1, 1 - p)
                    gn2_stats(t - 1, 1 - p)
                    gn2_spread(t - 1, 1 - p)
                if a:
                    k_partial_max(t, p)
                if b:
                    gn2_var(t - 1, 1 - p)
                if a:
                    k_maximum(t, p)
                    q_subtract(t, p)
                    k_subtract(t, p)
                if b:
                    route_first(t - 1, 1 - p)
                    image_low(t - 1, 1 - p)
                    route_second(t - 1, 1 - p)
                if c:
                    residual2(t - 2, p, 0)
                if a:
                    q_sums(t, p)
                if b:
                    gates(t - 1, 1 - p)
                if a:
                    context_scale(t, p)
                if b:
                    if isinstance(t, int) and t == 1:
                        dve.wait_ge(experts_ready, EXPERT_FILLS)
                    filters(t - 1, 1 - p)
                if a:
                    mix_evacuate(t, p)
                    if not (isinstance(t, int) and t + 1 >= B):
                        gn1_stats(t + 1, 1 - p)
                        gn1_spread(t + 1, 1 - p)
                        gn1_var(t + 1, 1 - p)
                if c:
                    residual2(t - 2, p, 1)

            gn1_stats(0, 0)
            gn1_spread(0, 0)
            gn1_var(0, 0)
            run_steps(dve, step)

        @block.tensor
        def _(pe):
            mm = nc.tensor.matmul
            tr = nc.tensor.transpose
            pe.wait_ge(pool_consts, 1)
            pe.wait_ge(consts_loaded, CONSTS)
            for s in range(3):
                tr(ps_y[:, tile(s)], wqkv_raw[:, s, :], ident[:, :])
            tr(ps_y[:, 512:512 + RC], rconv_raw[:, :], ident[0:RC, 0:RC]).then_inc(setup_pe, 1)
            tr(ps_att[:, 0:C], wout_raw[:, :], ident[:, :])
            tr(ps_att[0:MEM, 128:256], mem_c[:, 0, :], ident[:, :])
            tr(ps_att[0:MEM, 256:384], mem_c[:, 1, :], ident[:, :]).then_inc(setup_pe, 1)
            pe.wait_ge(setup_dve, 2)
            for ch in range(RCH):
                for k in range(K):
                    last = tr(ps_y[:, 512 * ch + 128 * k:512 * ch + 128 * k + 128], fc_raw[:, k, tile(ch)], ident[:, :])
                last.then_inc(setup_pe, 1)
            pe.wait_ge(setup_dve, 4)

            def expert_transposes():
                pe.wait_ge(experts_loaded, 16)
                n = 0
                for k in range(K):
                    by_tap = expert_raw[:, k, :].rearrange("o (c t) -> o t c", t=TAPS)
                    for first in range(0, TAPS, 4):
                        if n >= 2:
                            pe.wait_ge(experts_ready, n - 1)
                        for tap in range(first, min(first + 4, TAPS)):
                            last = tr(ps_conv[n % 2][:, tile(tap - first)], by_tap[:, tap, :], ident[:, :])
                        last.then_inc(expert_tiles, 1)
                        n += 1

            def gn1_mean(b, p):
                pe.wait_ge(meanvar1_done, b + 1)
                if past(b, 1):
                    pe.wait_ge(ssq1_done, b)
                if past(b, 2):
                    pe.wait_ge(route_z_done, b - 1)
                mm(ps_stat[:, 0:1], group_avg[:, :], meanvar1[:, 0:1], start=True, stop=True).then_inc(gmean1_ps, 1)

            def gn1_var(b, p):
                pe.wait_ge(spread1_done, b + 1)
                mm(ps_stat[:, 0:1], group_avg[:, :], spread1[:, :], start=True, stop=True).then_inc(gvar1_ps, 1)

            def squares1(b, p):
                pe.wait_ge(x1_sq_done, b + 1)
                pe.wait_ge(gvar1_done, b + 1)
                for t in range(NT):
                    last = mm(ps_stat[:, t:t + 1], x1_sq[:, tile(t)], ones[:, 0:1], start=True, stop=True)
                last.then_inc(ssq1_ps, 1)

            def project(b, p, t):
                if t == 0:
                    pe.wait_ge(x1_lo_done, b + 1)
                    if past(b, 1):
                        pe.wait_ge(q_t_done, 2 * b)
                if t >= 2:
                    pe.wait_ge(qkv_done, NT * b + t - 1)
                o = ps_qkv[t % 2][:, 0:QKV]
                mm(o, x1_hi[:, tile(t)], wqkv_hi[:, :], start=True, stop=False)
                mm(o, x1_hi[:, tile(t)], wqkv_lo[:, :], start=False, stop=False)
                mm(o, x1_lo[:, tile(t)], wqkv_hi[:, :], start=False, stop=True).then_inc(qkv_ps, 1)

            def k_part_transpose(b, p):
                pe.wait_ge(k_part_done, b + 1)
                if past(b, 1):
                    pe.wait_ge(mix_done, b)
                tr(ps_att[:, 0:128], k_max_part[:, :], ident[:, :]).then_inc(k_part_ps, 1)

            def k_shift(b, p):
                pe.wait_ge(k_diag_done, b + 1)
                mm(ps_att[:, 0:HID], ones_r[:, :], k_diag[:, :], start=True, stop=True).then_inc(k_shift_ps, 1)

            def contexts(b, p):
                pe.wait_ge(memk_exp_done, b + 1)
                pe.wait_ge(k_exp_done, b + 1)
                mm(ps_att[:, 0:VEXT], memk_exp[:, :], memv_t[:, :], start=True, stop=False)
                for t in range(NT):
                    last = mm(ps_att[:, 0:VEXT], k_exp[:, t, :], qkv[:, t, 2 * HID:3 * HID + 2], start=False, stop=(t == NT - 1))
                last.then_inc(context_ps, 1)

            def context_transpose(b, p):
                pe.wait_ge(context_done, b + 1)
                tr(ps_att[:, 0:HID], context[:, :], ident[:, :]).then_inc(context_t_ps, 1)

            def mixes(b, p):
                pe.wait_ge(context_t_done, b + 1)
                mm(ps_att[:, 0:C], context_t[:, :], wout_t[:, :], start=True, stop=True).then_inc(mix_ps, 1)

            def q_transpose(b, p):
                pe.wait_ge(q_norm_done, b + 1)
                pe.wait_ge(qkv_done, NT * (b + 1))
                for h in range(2):
                    for t in range(NT // 2):
                        tt = NT // 2 * h + t
                        last = tr(ps_qkv[h][:, tile(t)], q_exp[:, HEADS * tt:HEADS * (tt + 1), :].rearrange("p h d -> p (h d)"), ident[:, :])
                    last.then_inc(q_t_ps, 1)

            def outputs(b, p):
                pe.wait_ge(mix_done, b + 1)
                pe.wait_ge(q_t_done, 2 * (b + 1))
                if past(b, 1):
                    pe.wait_ge(x2_done, b)
                for t in range(NT):
                    last = mm(ps_y[:, tile(t)], q_t[p][:, tile(t)], mix[p][:, :], start=True, stop=True)
                last.then_inc(y_ps, 1)

            def y_transpose(b, p):
                pe.wait_ge(y_scaled_done, b + 1)
                for t in range(NT):
                    last = tr(ps_y[:, tile(t)], y_scaled[:, t, :], ident[:, :])
                last.then_inc(y_t_ps, 1)

            def gn2_mean(b, p):
                pe.wait_ge(meanvar2_done, b + 1)
                if past(b, 1):
                    pe.wait_ge(route_z_done, b)
                if not (isinstance(b, int) and b == B - 1):
                    pe.wait_ge(ssq1_done, b + 2)
                mm(ps_stat[:, 0:1], group_avg[:, :], meanvar2[:, 0:1], start=True, stop=True).then_inc(gmean2_ps, 1)

            def gn2_var(b, p):
                pe.wait_ge(spread2_done, b + 1)
                mm(ps_stat[:, 0:1], group_avg[:, :], spread2[:, :], start=True, stop=True).then_inc(gvar2_ps, 1)

            def route_first(b, p):
                pe.wait_ge(route_prod_done, b + 1)
                pe.wait_ge(gvar2_done, b + 1)
                flat = route_prod[:, :, :].rearrange("p r s -> p (r s)")
                for ch in range(RCH):
                    last = mm(ps_stat[:, ch:ch + 1], flat[:, tile(ch)], ones[:, 0:1], start=True, stop=True)
                last.then_inc(route_y_ps, 1)

            def route_second(b, p):
                pe.wait_ge(route_y_done, b + 1)
                for k in range(K):
                    for ch in range(RCH):
                        last = mm(ps_stat[:, k:k + 1], fc_t[:, ch, k * C:(k + 1) * C], route_y[:, ch:ch + 1],
                                  start=(ch == 0), stop=(ch == RCH - 1))
                last.then_inc(route_z_ps, 1)

            def convolution(b, p):
                pe.wait_ge(w_lo_done, b + 1)
                pe.wait_ge(pad_lo_done, b + 1)
                pe.wait_ge(pad_hi_done, b + 1)
                for h in range(2):
                    if past(b, 1):
                        pe.wait_ge(result_done, 2 * (b - 1) + h + 1)
                    n = 0
                    for tap in range(TAPS):
                        di, dj = tap // KW, tap % KW
                        rows, cols = slice(HH * h + di, HH * h + di + HH), slice(dj, dj + W)
                        for weight, pixels in ((w_hi[p], pad_hi[p]), (w_hi[p], pad_lo[p]), (w_lo[p], pad_hi[p])):
                            last = mm(ps_conv[h][:, :], weight[:, tap, :], pixels[:, rows, cols],
                                      start=(n == 0), stop=(n == 3 * TAPS - 1))
                            n += 1
                            if n == 3 * TAPS:
                                last.then_inc(conv_ps, 1)
                            yield

            def step(t, p, a, b, c):
                products = convolution(t - 2, p) if c else iter(())

                def conv(n):
                    for _ in range(n):
                        next(products, None)

                if b:
                    outputs(t - 1, 1 - p)
                conv(4)
                if a:
                    squares1(t, p)
                conv(6)
                if b:
                    y_transpose(t - 1, 1 - p)
                for tt in range(NT):
                    if a:
                        project(t, p, tt)
                    conv(1)
                if b:
                    gn2_mean(t - 1, 1 - p)
                conv(2)
                if b:
                    gn2_var(t - 1, 1 - p)
                conv(2)
                if a:
                    k_part_transpose(t, p)
                    conv(2)
                    k_shift(t, p)
                conv(5)
                if b:
                    route_first(t - 1, 1 - p)
                conv(3)
                if b:
                    route_second(t - 1, 1 - p)
                if a:
                    contexts(t, p)
                    conv(3)
                    context_transpose(t, p)
                    conv(3)
                    mixes(t, p)
                    conv(2)
                    q_transpose(t, p)
                conv(6)
                if a and not (isinstance(t, int) and t + 1 >= B):
                    gn1_mean(t + 1, 1 - p)
                    conv(3)
                    gn1_var(t + 1, 1 - p)
                conv(54)
                if isinstance(t, int) and t == 0:
                    expert_transposes()

            gn1_mean(0, 0)
            gn1_var(0, 0)
            run_steps(pe, step)


_INS = ['x', 'L0_conv_g1', 'L0_conv_w_qkv', 'L0_conv_mem_kv', 'L0_conv_w_out', 'L0_conv_b_out', 'L0_conv_g2',
        'L1_conv_expert_weight', 'L1_conv_rconv_w', 'L1_conv_rconv_b', 'L1_conv_fc_w', 'L1_conv_fc_b']


def kernel(**inputs):
    import numpy as _np
    import concourse.bacc as _bacc
    from concourse import mybir as _mybir
    from concourse.bass_utils import run_bass_kernel_spmd as _run

    nc = _bacc.Bacc("TRN2", target_bir_lowering=False, num_devices=1)
    arrays, args = {}, []
    for name in _INS:
        a = _np.ascontiguousarray(inputs[name])
        arrays[f"in_{name}_dram"] = a
        args.append(nc.dram_tensor(f"in_{name}_dram", a.shape, _mybir.dt.from_np(a.dtype), kind="ExternalInput").ap())
    shape = inputs["x"].shape
    args.append(nc.dram_tensor("out_0_dram", shape, _mybir.dt.float32, kind="ExternalOutput").ap())
    attention_condconv_kernel(nc, *args)
    r = _run(nc, [arrays], core_ids=[0])
    return r.results[0]["out_0_dram"]
```

```python
from contextlib import ExitStack

import concourse.bass as bass
from concourse import mybir

F32 = mybir.dt.float32
F32R = mybir.dt.float32r
ALU = mybir.AluOpType
ACT = mybir.ActivationFunctionType
AX = mybir.AxisListType


def attention_condconv_kernel(
    nc: bass.Bass,
    x: bass.AP,
    g1: bass.AP,
    w_qkv: bass.AP,
    mem_kv: bass.AP,
    w_out: bass.AP,
    b_out: bass.AP,
    g2: bass.AP,
    expert_weight: bass.AP,
    rconv_w: bass.AP,
    rconv_b: bass.AP,
    fc_w: bass.AP,
    fc_b: bass.AP,
    out: bass.AP,
):
    B, C, H, W = x.shape
    N = H * W
    NT = N // 128
    _, HEADS, DH, MEM = mem_kv.shape
    HID = HEADS * DH
    K, CO, _, KH, KW = expert_weight.shape
    TAPS = KH * KW
    RC = rconv_w.shape[0]
    SP = 4
    CELL = (H // SP) * (W // SP)
    RF = RC * SP * SP
    GC = C // 32
    PH, PW = H + 2, W + 2
    HH = H // 2
    QKV = 3 * HID
    VEXT = HID + 2
    GN_EPS, NORM_MIN = 1e-5, 1e-12
    assert C == 128 and HID == 128 and CO == 128 and HH * W == 512 and RF <= 512 and B % 2 == 0

    x_d = x.rearrange("b c h w -> b c (h w)")
    out_d = out.rearrange("b c h w -> b c (h w)")

    ctx = ExitStack()
    with ctx:
        def sb(name, shape, dt=F32):
            return ctx.enter_context(nc.sbuf_tensor(name, shape, dt))

        def psum(name, shape):
            return ctx.enter_context(nc.psum_tensor(name, shape, F32))

        def sem(name):
            return ctx.enter_context(nc.semaphore(name))

        ident = sb("ident", [128, 128])
        ones = sb("ones", [128, 128])
        ones_r = sb("ones_r", [128, 128], F32R)
        group_avg = sb("group_avg", [128, 128])
        head_mask = sb("head_mask", [128, 128])
        minus_half = sb("minus_half", [128, NT])
        wqkv_raw = sb("wqkv_raw", [128, 3, C])
        wqkv_t = sb("wqkv_t", [128, QKV])
        wqkv_hi = sb("wqkv_hi", [128, QKV], F32R)
        wqkv_lo = sb("wqkv_lo", [128, QKV], F32R)
        wout_raw = sb("wout_raw", [128, HID])
        wout_t = sb("wout_t", [128, C])
        bias_share = sb("bias_share", [128, C])
        bias_raw = sb("bias_raw", [128, C])
        g1_c = sb("g1_c", [128, 1])
        g2_c = sb("g2_c", [128, 1])
        mem_c = sb("mem_c", [128, 2, MEM])
        memk_max = sb("memk_max", [128, 1])
        memk_diag = sb("memk_diag", [128, 128])
        memk_t = sb("memk_t", [MEM, HID])
        memv_t = sb("memv_t", [MEM, VEXT])
        expert_raw = sb("expert_raw", [128, K, C * TAPS])
        experts = sb("experts", [128, K, TAPS * CO])
        rconv_raw = sb("rconv_raw", [RC, C])
        rconv_t = sb("rconv_t", [128, RC])
        rconv_bias = sb("rconv_bias", [128, RC])
        fc = sb("fc", [128, K, RF])
        fc_bias = sb("fc_bias", [128, K])

        xa = [sb(f"xa{p}", [128, N]) for p in range(2)]
        stats1 = sb("stats1", [128, 2, 6])
        meanvar1 = sb("meanvar1", [128, 2])
        nmean1 = sb("nmean1", [128, 1])
        dev1 = sb("dev1", [128, 1])
        spread1 = sb("spread1", [128, 1])
        gvar1 = sb("gvar1", [128, 1])
        rstd1 = [sb(f"rstd1_{p}", [128, 1]) for p in range(2)]
        shift1 = [sb(f"shift1_{p}", [128, 1]) for p in range(2)]
        x1 = sb("x1", [128, N])
        x1_sq = sb("x1_sq", [128, N])
        x1_hi = sb("x1_hi", [128, N], F32R)
        x1_lo = sb("x1_lo", [128, N], F32R)
        ssq1 = sb("ssq1", [128, NT])
        scale1 = sb("scale1", [128, NT])
        qkv = sb("qkv", [128, NT, QKV + 2])
        k_max_part = sb("k_max_part", [128, HID])
        k_max = sb("k_max", [128, 1])
        k_diag = sb("k_diag", [128, 128], F32R)
        k_exp = sb("k_exp", [128, NT, HID])
        memk_exp = sb("memk_exp", [MEM, HID])
        q_max = sb("q_max", [128, NT * HEADS])
        q_exp = sb("q_exp", [128, NT * HEADS, DH])
        q_sum = sb("q_sum", [128, NT * HEADS])
        q_rsum = sb("q_rsum", [128, NT * HEADS])
        k_rsum = sb("k_rsum", [128, 1])
        context = sb("context", [128, HID])
        context_t = sb("context_t", [128, HID])
        q_t = [sb(f"q_t{p}", [128, N]) for p in range(2)]
        mix = [sb(f"mix{p}", [128, C]) for p in range(2)]

        xb = [sb(f"xb{p}", [128, N]) for p in range(2)]
        y_sq = sb("y_sq", [128, N])
        ssq2_sum = sb("ssq2_sum", [128, NT])
        ssq2 = sb("ssq2", [128, NT])
        scale2 = sb("scale2", [128, NT])
        y_scaled = sb("y_scaled", [128, NT, C])
        x2 = [sb(f"x2_{p}", [128, N]) for p in range(2)]
        stats2 = sb("stats2", [128, 2, 6])
        meanvar2 = sb("meanvar2", [128, 2])
        nmean2 = sb("nmean2", [128, 1])
        dev2 = sb("dev2", [128, 1])
        spread2 = sb("spread2", [128, 1])
        gvar2 = sb("gvar2", [128, 1])
        rstd2 = sb("rstd2", [128, 1])
        pooled = sb("pooled", [128, SP * SP])
        pooled_c = sb("pooled_c", [128, SP * SP])
        pooled_n = sb("pooled_n", [128, SP * SP])
        route_prod = sb("route_prod", [128, RC, SP * SP])
        route_y = sb("route_y", [128, RF])
        route_terms = sb("route_terms", [128, K, RF])
        route_sum = sb("route_sum", [128, K])
        route_z = sb("route_z", [128, K])
        route_zr = sb("route_zr", [128, K])
        route_e = sb("route_e", [128, K])
        route_d = sb("route_d", [128, K])
        gate = sb("gate", [128, K])
        gate_n = sb("gate_n", [128, K])
        w_first = sb("w_first", [128, TAPS * CO])
        w_second = sb("w_second", [128, TAPS * CO])
        w_full = sb("w_full", [128, TAPS * CO])
        w_hi = [sb(f"w_hi{p}", [128, TAPS, CO], F32R) for p in range(2)]
        w_lo = [sb(f"w_lo{p}", [128, TAPS, CO], F32R) for p in range(2)]
        pad_hi = [sb(f"pad_hi{p}", [128, PH, PW], F32R) for p in range(2)]
        pad_lo = [sb(f"pad_lo{p}", [128, PH, PW], F32R) for p in range(2)]

        result = [sb(f"result{p}", [128, N]) for p in range(2)]

        ps_conv = [psum(f"ps_conv{h}", [128, 512]) for h in range(2)]
        ps_qkv = [psum(f"ps_qkv{h}", [128, 512]) for h in range(2)]
        ps_y = psum("ps_y", [128, 1024])
        ps_att = psum("ps_att", [128, 512])
        ps_stat = psum("ps_stat", [128, 512])

        consts_loaded = sem("consts_loaded")
        experts_loaded = sem("experts_loaded")
        pool_zeros = sem("pool_zeros")
        pool_consts = sem("pool_consts")
        setup_pe = sem("setup_pe")
        setup_dve = sem("setup_dve")
        setup_act = sem("setup_act")
        expert_tiles = sem("expert_tiles")
        experts_ready = sem("experts_ready")
        xa_loaded = [sem(f"xa_loaded{p}") for p in range(2)]
        xb_loaded = [sem(f"xb_loaded{p}") for p in range(2)]
        stored = [sem(f"stored{p}") for p in range(2)]

        stats1_done = sem("stats1_done")
        meanvar1_done = sem("meanvar1_done")
        gmean1_ps = sem("gmean1_ps")
        nmean1_done = sem("nmean1_done")
        dev1_done = sem("dev1_done")
        spread1_done = sem("spread1_done")
        gvar1_ps = sem("gvar1_ps")
        gvar1_done = sem("gvar1_done")
        rstd1_done = sem("rstd1_done")
        shift1_done = sem("shift1_done")
        x1_started = sem("x1_started")
        stats1_read = sem("stats1_read")
        stats2_read = sem("stats2_read")
        x1_done = sem("x1_done")
        x1_sq_done = sem("x1_sq_done")
        x1_hi_done = sem("x1_hi_done")
        x1_lo_done = sem("x1_lo_done")
        ssq1_ps = sem("ssq1_ps")
        ssq1_done = sem("ssq1_done")
        scale1_done = sem("scale1_done")
        qkv_ps = sem("qkv_ps")
        qkv_done = sem("qkv_done")
        k_part_done = sem("k_part_done")
        k_part_ps = sem("k_part_ps")
        k_max_done = sem("k_max_done")
        k_diag_done = sem("k_diag_done")
        k_shift_ps = sem("k_shift_ps")
        k_sub_done = sem("k_sub_done")
        memk_sub_done = sem("memk_sub_done")
        k_exp_done = sem("k_exp_done")
        memk_exp_done = sem("memk_exp_done")
        q_max_done = sem("q_max_done")
        q_sub_done = sem("q_sub_done")
        q_exp_done = sem("q_exp_done")
        q_sum_done = sem("q_sum_done")
        q_rsum_done = sem("q_rsum_done")
        q_norm_done = sem("q_norm_done")
        context_ps = sem("context_ps")
        k_rsum_done = sem("k_rsum_done")
        context_done = sem("context_done")
        context_t_ps = sem("context_t_ps")
        context_t_done = sem("context_t_done")
        mix_ps = sem("mix_ps")
        mix_done = sem("mix_done")
        q_t_ps = sem("q_t_ps")
        q_t_done = sem("q_t_done")

        y_ps = sem("y_ps")
        ssq2_sum_done = sem("ssq2_sum_done")
        ssq2_done = sem("ssq2_done")
        scale2_done = sem("scale2_done")
        y_scaled_done = sem("y_scaled_done")
        y_t_ps = sem("y_t_ps")
        x2_done = sem("x2_done")
        stats2_done = sem("stats2_done")
        meanvar2_done = sem("meanvar2_done")
        pooled_done = sem("pooled_done")
        gmean2_ps = sem("gmean2_ps")
        nmean2_done = sem("nmean2_done")
        dev2_done = sem("dev2_done")
        spread2_done = sem("spread2_done")
        gvar2_ps = sem("gvar2_ps")
        gvar2_done = sem("gvar2_done")
        rstd2_done = sem("rstd2_done")
        pooled_c_done = sem("pooled_c_done")
        pooled_n_done = sem("pooled_n_done")
        route_prod_done = sem("route_prod_done")
        route_y_ps = sem("route_y_ps")
        route_y_done = sem("route_y_done")
        route_sum_done = sem("route_sum_done")
        route_z_done = sem("route_z_done")
        route_zr_done = sem("route_zr_done")
        route_e_done = sem("route_e_done")
        route_d_done = sem("route_d_done")
        gate_done = sem("gate_done")
        gate_n_done = sem("gate_n_done")
        w_first_done = sem("w_first_done")
        w_second_done = sem("w_second_done")
        w_full_done = sem("w_full_done")
        w_hi_done = sem("w_hi_done")
        w_lo_done = sem("w_lo_done")
        pad_hi_done = sem("pad_hi_done")
        pad_lo_done = sem("pad_lo_done")
        conv_ps = sem("conv_ps")
        result_done = sem("result_done")

        def tile(t):
            return slice(128 * t, 128 * t + 128)

        def half(h):
            return slice(512 * h, 512 * h + 512)

        def interior(pad, lo=0, hi=H):
            return pad[:, 1 + lo:1 + hi, 1:1 + W]

        def image(flat, lo=0, hi=H):
            return flat[:, lo * W:hi * W].rearrange("p (h w) -> p h w", w=W)

        def past(b, n):
            return not isinstance(b, int) or b >= n

        def slot_count(b, p):
            return 8 * (b - p) + 16

        OLDEST = 3
        STEPS = B + OLDEST
        FIRST, LAST = OLDEST + 2, B - 1

        def run_steps(eng, step):
            for t in range(FIRST):
                step(t, t % 2)
            with eng.Fori(FIRST, LAST - 1, 2) as i:
                step(i, FIRST % 2)
                step(i + 1, 1 - FIRST % 2)
            for t in range(LAST, STEPS):
                step(t, t % 2)

        def do(part, t, p, age, *args):
            b = t - age
            if not isinstance(b, int) or 0 <= b < B:
                part(b, (p - age) % 2, *args)

        block = ctx.enter_context(nc.Block())

        @block.sync
        def _(sp):
            def load_xa(b, p):
                if past(b, 2):
                    sp.wait_ge(x1_done, b - 1)
                    sp.wait_ge(x1_hi_done, b - 1)
                    sp.wait_ge(x1_sq_done, b - 1)
                sp.dma_start(xa[p][:, :], x_d[b]).then_inc(xa_loaded[p], 16)

            def load_xb(b, p):
                if past(b, 2):
                    sp.wait_ge(x2_done, b - 1)
                sp.dma_start(xb[p][:, :], x_d[b]).then_inc(xb_loaded[p], 16)

            def store(b, p):
                sp.wait_ge(result_done, 2 * (b + 1))
                sp.dma_start(out_d[b], result[p][:, :]).then_inc(stored[p], 16)

            load_xa(0, 0)
            sp.dma_start(wqkv_raw[:, :, :], w_qkv.rearrange("(s o) c -> o s c", s=3)).then_inc(consts_loaded, 16)
            sp.dma_start(g1_c[:, :], g1.rearrange("(c a) -> c a", a=1)).then_inc(consts_loaded, 16)
            sp.dma_start(mem_c[:, :, :], mem_kv.rearrange("s h d m -> (h d) s m")).then_inc(consts_loaded, 16)
            sp.dma_start(wout_raw[:, :], w_out).then_inc(consts_loaded, 16)
            sp.dma_start(g2_c[:, :], g2.rearrange("(c a) -> c a", a=1)).then_inc(consts_loaded, 16)
            sp.dma_start(bias_raw[:, :], b_out.rearrange("(a c) -> a c", a=1).to_broadcast((128, C))).then_inc(consts_loaded, 16)
            sp.dma_start(rconv_raw[:, :], rconv_w).then_inc(consts_loaded, 16)
            sp.dma_start(rconv_bias[:, :], rconv_b.rearrange("(a r) -> a r", a=1).to_broadcast((128, RC))).then_inc(consts_loaded, 16)
            sp.dma_start(fc[:, :, :], fc_w.rearrange("(k c) j -> c k j", k=K)).then_inc(consts_loaded, 16)
            sp.dma_start(fc_bias[:, :], fc_b.rearrange("(k c) -> c k", k=K), allow_slow_non_contiguous=True).then_inc(consts_loaded, 16)
            sp.dma_start(expert_raw[:, :, :], expert_weight.rearrange("k o c i j -> o k (c i j)")).then_inc(experts_loaded, 16)

            def step(t, p):
                do(load_xa, t, p, -1)
                do(load_xb, t, p, 1)
                do(store, t, p, 3)

            run_steps(sp, step)
            for p in range(2):
                sp.wait_ge(stored[p], 16 * (B // 2))

        CONSTS = 16 * 10
        EXPERT_FILLS = K * -(-TAPS // 4)

        @block.gpsimd
        def _(pool):
            nc.gpsimd.memset(ident[:, :], 0.0)
            nc.gpsimd.memset(group_avg[:, :], 1.0 / GC)
            nc.gpsimd.memset(head_mask[:, :], float(DH) ** -0.5)
            nc.gpsimd.memset(memv_t[:, :], 1.0)
            for p in range(2):
                nc.gpsimd.memset(pad_hi[p][:, :, :].bitcast(F32), 0.0)
                nc.gpsimd.memset(pad_lo[p][:, :, :].bitcast(F32), 0.0)
            nc.gpsimd.memset(qkv[:, :, QKV:QKV + 2], 1.0)
            nc.gpsimd.memset(ones[:, :], 1.0).then_inc(pool_zeros, 1)
            pool.wait_ge(pool_zeros, 1)
            nc.gpsimd.affine_select(out=ident[:, :], in_=ident[:, :], compare_op=ALU.not_equal, fill=1.0,
                                    base=0, pattern=[[-1, 128]], channel_multiplier=1)
            for mask, size in ((group_avg, GC), (head_mask, DH)):
                blocks = mask[:, :].rearrange("p (g j) -> p g j", j=size)
                nc.gpsimd.affine_select(out=blocks, in_=blocks, compare_op=ALU.is_ge, fill=0.0, base=0,
                                        pattern=[[-size, 128 // size], [0, size]], channel_multiplier=1)
            nc.gpsimd.memset(minus_half[:, :], -0.5).then_inc(pool_zeros, 1)
            pool.wait_ge(pool_zeros, 2)
            for mask, size in ((group_avg, GC), (head_mask, DH)):
                blocks = mask[:, :].rearrange("p (g j) -> p g j", j=size)
                last = nc.gpsimd.affine_select(out=blocks, in_=blocks, compare_op=ALU.is_ge, fill=0.0, base=size - 1,
                                               pattern=[[size, 128 // size], [0, size]], channel_multiplier=-1)
            last.then_inc(pool_consts, 1)

            def gn1_rstd(b, p):
                pool.wait_ge(gvar1_done, b + 1)
                if past(b, 2):
                    pool.wait_ge(x1_done, b - 1)
                    pool.wait_ge(x1_hi_done, b - 1)
                nc.gpsimd.tensor_tensor(rstd1[p][:, :], gvar1[:, :], minus_half[:, 0:1], ALU.pow).then_inc(rstd1_done, 1)

            def gn1_shift(b, p):
                pool.wait_ge(rstd1_done, b + 1)
                nc.gpsimd.tensor_tensor(shift1[p][:, :], nmean1[:, :], rstd1[p][:, :], ALU.mult).then_inc(shift1_done, 1)

            def normalise1(b, p):
                pool.wait_ge(xa_loaded[p], slot_count(b, p))
                if past(b, 1):
                    pool.wait_ge(x1_lo_done, b)
                pool.wait_ge(shift1_done, b + 1).then_inc(x1_started, 1)
                nc.gpsimd.tensor_scalar(x1[:, :], xa[p][:, :], rstd1[p][:, :], shift1[p][:, :], ALU.mult, ALU.add).then_inc(x1_done, 1)

            def low1(b, p):
                pool.wait_ge(x1_done, b + 1)
                pool.wait_ge(x1_hi_done, b + 1)
                if past(b, 1):
                    pool.wait_ge(qkv_ps, NT * b)
                nc.gpsimd.tensor_tensor(x1_lo[:, :], x1[:, :], x1_hi[:, :].bitcast(F32), ALU.subtract).then_inc(x1_lo_done, 1)

            def rms1(b, p):
                pool.wait_ge(ssq1_done, b + 1)
                if past(b, 1):
                    pool.wait_ge(qkv_done, NT * b)
                nc.gpsimd.tensor_tensor(scale1[:, :], ssq1[:, :], minus_half[:, :], ALU.pow).then_inc(scale1_done, 1)

            def q_normalise(b, p):
                pool.wait_ge(q_rsum_done, b + 1)
                nc.gpsimd.tensor_tensor(q_exp[:, :, :], q_exp[:, :, :],
                                        q_rsum[:, :].unsqueeze(2).to_broadcast((128, NT * HEADS, DH)),
                                        ALU.mult).then_inc(q_norm_done, 1)

            def rms2(b, p):
                pool.wait_ge(ssq2_done, b + 1)
                if past(b, 1):
                    pool.wait_ge(y_scaled_done, b)
                nc.gpsimd.tensor_tensor(scale2[:, :], ssq2[:, :], minus_half[:, :], ALU.pow).then_inc(scale2_done, 1)

            def gn2(b, p):
                pool.wait_ge(gvar2_done, b + 1)
                if past(b, 1):
                    pool.wait_ge(gate_n_done, b)
                nc.gpsimd.tensor_tensor(rstd2[:, :], gvar2[:, :], minus_half[:, 0:1], ALU.pow).then_inc(rstd2_done, 1)

            def pooled_normalise(b, p):
                if not past(b, 1):
                    pool.wait_ge(setup_dve, 1)
                pool.wait_ge(pooled_c_done, b + 1)
                pool.wait_ge(rstd2_done, b + 1)
                nc.gpsimd.tensor_tensor(pooled_n[:, :], pooled_c[:, :], rstd2[:, :].to_broadcast((128, SP * SP)), ALU.mult).then_inc(pooled_n_done, 1)

            def routing_products(b, p):
                pool.wait_ge(pooled_n_done, b + 1)
                if past(b, 1):
                    pool.wait_ge(route_y_ps, b)
                nc.gpsimd.tensor_tensor(route_prod[:, :, :],
                                        rconv_t[:, :].unsqueeze(2).to_broadcast((128, RC, SP * SP)),
                                        pooled_n[:, :].unsqueeze(1).to_broadcast((128, RC, SP * SP)),
                                        ALU.mult).then_inc(route_prod_done, 1)

            def filters_low(b, p):
                pool.wait_ge(w_full_done, b + 1)
                pool.wait_ge(w_hi_done, b + 1)
                if past(b, 2):
                    pool.wait_ge(conv_ps, 2 * (b - 1))
                nc.gpsimd.tensor_tensor(w_lo[p][:, :, :].rearrange("p t o -> p (t o)"), w_full[:, :],
                                        w_hi[p][:, :, :].bitcast(F32).rearrange("p t o -> p (t o)"),
                                        ALU.subtract).then_inc(w_lo_done, 1)

            def step(t, p):
                do(gn1_shift, t, p, 1)
                do(normalise1, t, p, 1)
                do(q_normalise, t, p, 2)
                do(low1, t, p, 1)
                do(gn2, t, p, 3)
                do(pooled_normalise, t, p, 3)
                do(routing_products, t, p, 3)
                do(rms1, t, p, 1)
                do(rms2, t, p, 2)
                do(filters_low, t, p, 3)
                do(gn1_rstd, t, p, 0)

            run_steps(pool, step)

        @block.scalar
        def _(act):
            act.wait_ge(pool_zeros, 1)
            nc.scalar.activation(ones_r[:, :], ones[:, :], ACT.Copy).then_inc(setup_act, 1)
            act.wait_ge(setup_dve, 1)
            nc.scalar.activation(wqkv_hi[:, :], wqkv_t[:, :], ACT.Copy).then_inc(setup_act, 1)

            def square1(b, p):
                act.wait_ge(shift1_done, b + 1)
                act.wait_ge(xa_loaded[p], slot_count(b, p))
                if past(b, 1):
                    act.wait_ge(ssq1_ps, b)
                nc.scalar.activation(x1_sq[:, :], xa[p][:, :], ACT.Square, bias=shift1[p][:, :], scale=rstd1[p][:, :]).then_inc(x1_sq_done, 1)

            def high1(b, p):
                act.wait_ge(shift1_done, b + 1)
                act.wait_ge(xa_loaded[p], slot_count(b, p))
                if past(b, 1):
                    act.wait_ge(qkv_ps, NT * b)
                    act.wait_ge(x1_lo_done, b)
                nc.scalar.activation(x1_hi[:, :], xa[p][:, :], ACT.Identity, bias=shift1[p][:, :], scale=rstd1[p][:, :]).then_inc(x1_hi_done, 1)

            def qkv_evacuate(b, p, t):
                if t == 0:
                    act.wait_ge(scale1_done, b + 1)
                    if past(b, 1):
                        act.wait_ge(k_sub_done, b)
                        act.wait_ge(q_sub_done, b)
                        act.wait_ge(context_ps, b)
                act.wait_ge(qkv_ps, NT * b + t + 1)
                nc.scalar.activation(qkv[:, t, 0:QKV], ps_qkv[t % 2][:, 0:QKV], ACT.Copy, scale=scale1[:, t:t + 1]).then_inc(qkv_done, 1)

            def memk_exponent(b, p):
                act.wait_ge(memk_sub_done, b + 1)
                nc.scalar.activation(memk_exp[:, :], memk_exp[:, :], ACT.Exp).then_inc(memk_exp_done, 1)

            def k_exponent(b, p):
                act.wait_ge(k_sub_done, b + 1)
                nc.scalar.activation(k_exp[:, :, :], k_exp[:, :, :], ACT.Exp).then_inc(k_exp_done, 1)

            def q_exponent(b, p):
                act.wait_ge(q_sub_done, b + 1)
                nc.scalar.activation(q_exp[:, :, :], q_exp[:, :, :], ACT.Exp).then_inc(q_exp_done, 1)

            def context_evacuate(b, p):
                act.wait_ge(context_t_ps, b + 1)
                if past(b, 1):
                    act.wait_ge(mix_ps, b)
                nc.scalar.activation(context_t[:, :], ps_att[:, 0:HID], ACT.Copy).then_inc(context_t_done, 1)

            def q_evacuate(b, p, h):
                if past(b, 2):
                    act.wait_ge(y_ps, b - 1)
                act.wait_ge(q_t_ps, 2 * b + h + 1)
                nc.scalar.activation(q_t[p][:, half(h)], ps_qkv[h][:, :], ACT.Copy).then_inc(q_t_done, 1)

            def squares2(b, p):
                act.wait_ge(y_ps, b + 1)
                if past(b, 1):
                    act.wait_ge(ssq2_done, b)
                    act.wait_ge(ssq2_sum_done, b)
                for t in range(NT):
                    last = nc.scalar.activation(y_sq[:, tile(t)], ps_y[:, tile(t)], ACT.Square, accum_out=ssq2_sum[:, t:t + 1])
                last.then_inc(ssq2_sum_done, 1)

            def image_high(b, p):
                act.wait_ge(nmean2_done, b + 1)
                if past(b, 2):
                    act.wait_ge(conv_ps, 2 * (b - 1))
                nc.scalar.activation(interior(pad_hi[p]), image(x2[p]), ACT.Identity, bias=nmean2[:, :]).then_inc(pad_hi_done, 1)

            def gate_exponent(b, p):
                act.wait_ge(route_zr_done, b + 1)
                nc.scalar.activation(route_e[:, :], route_zr[:, :], ACT.Exp, scale=-1.0).then_inc(route_e_done, 1)

            def filters_first(b, p):
                if not past(b, 1):
                    act.wait_ge(experts_ready, EXPERT_FILLS)
                act.wait_ge(gate_n_done, b + 1)
                if past(b, 1):
                    act.wait_ge(w_second_done, b)
                nc.scalar.activation(w_first[:, :], experts[:, 0, :], ACT.Copy, scale=gate_n[:, 0:1]).then_inc(w_first_done, 1)

            def filters_high(b, p):
                act.wait_ge(w_full_done, b + 1)
                if past(b, 2):
                    act.wait_ge(conv_ps, 2 * (b - 1))
                nc.scalar.activation(w_hi[p][:, :, :].rearrange("p t o -> p (t o)"), w_full[:, :], ACT.Copy).then_inc(w_hi_done, 1)

            def experts_evacuate():
                n = 0
                for k in range(K):
                    for first in range(0, TAPS, 4):
                        taps = min(4, TAPS - first)
                        act.wait_ge(expert_tiles, n + 1)
                        last = nc.scalar.activation(experts[:, k, first * CO:(first + taps) * CO],
                                                    ps_conv[n % 2][:, 0:taps * CO], ACT.Copy).then_inc(experts_ready, 1)
                        n += 1

            def step(t, p):
                do(filters_first, t, p, 3)
                do(qkv_evacuate, t, p, 1, 3)
                do(qkv_evacuate, t, p, 1, 4)
                do(qkv_evacuate, t, p, 1, 5)
                do(qkv_evacuate, t, p, 1, 6)
                do(qkv_evacuate, t, p, 1, 7)
                do(filters_high, t, p, 3)
                do(memk_exponent, t, p, 1)
                do(q_exponent, t, p, 1)
                do(k_exponent, t, p, 1)
                do(square1, t, p, 0)
                do(high1, t, p, 0)
                do(context_evacuate, t, p, 1)
                do(q_evacuate, t, p, 1, 0)
                do(q_evacuate, t, p, 1, 1)
                do(image_high, t, p, 2)
                do(squares2, t, p, 1)
                if isinstance(t, int) and t == 1:
                    experts_evacuate()
                do(qkv_evacuate, t, p, 0, 0)
                do(gate_exponent, t, p, 2)
                do(qkv_evacuate, t, p, 0, 1)
                do(qkv_evacuate, t, p, 0, 2)

            run_steps(act, step)

        @block.vector
        def _(dve):
            v = nc.vector
            dve.wait_ge(consts_loaded, CONSTS)
            dve.wait_ge(setup_pe, 1)
            v.tensor_scalar(wqkv_t[:, :], ps_y[:, 0:QKV], g1_c[:, :], None, ALU.mult)
            v.tensor_copy(rconv_t[:, :], ps_y[:, 512:512 + RC]).then_inc(setup_dve, 1)
            dve.wait_ge(setup_act, 2)
            v.tensor_tensor(wqkv_lo[:, :], wqkv_t[:, :], wqkv_hi[:, :].bitcast(F32), ALU.subtract).then_inc(setup_dve, 1)

            dve.wait_ge(setup_pe, 2)
            v.tensor_copy(wout_t[:, :], ps_att[:, 0:C])
            v.tensor_copy(memk_t[:, :], ps_att[0:MEM, 128:256])
            v.tensor_copy(memv_t[:, 0:HID], ps_att[0:MEM, 256:384])
            v.tensor_scalar(bias_share[:, :], bias_raw[:, :], 1.0 / HEADS, None, ALU.mult)
            v.tensor_reduce(memk_max[:, :], mem_c[:, 0, :], AX.X, ALU.max).then_inc(setup_dve, 1)
            dve.wait_ge(setup_dve, 3)
            v.tensor_scalar(memk_diag[:, :], ident[:, :], memk_max[:, :], None, ALU.mult).then_inc(setup_dve, 1)
            dve.wait_ge(setup_dve, 4)

            def gn1_stats(b, p):
                dve.wait_ge(xa_loaded[p], slot_count(b, p))
                if past(b, 1):
                    dve.wait_ge(meanvar1_done, b)
                for h in range(2):
                    last = v.bn_stats(stats1[:, h, :], xa[p][:, half(h)])
                last.then_inc(stats1_done, 1)

            def gn1_aggregate(b, p):
                if past(b, 1):
                    dve.wait_ge(gmean1_ps, b)
                    dve.wait_ge(spread1_done, b)
                dve.wait_ge(stats1_done, b + 1).then_inc(stats1_read, 1)
                v.bn_aggr(meanvar1[:, :], stats1[:, :, :].rearrange("p h s -> p (h s)")).then_inc(meanvar1_done, 1)

            def gn1_mean(b, p):
                dve.wait_ge(gmean1_ps, b + 1)
                if past(b, 1):
                    dve.wait_ge(shift1_done, b)
                v.tensor_scalar(nmean1[:, :], ps_stat[:, 0:1], -1.0, None, ALU.mult).then_inc(nmean1_done, 1)

            def gn1_deviation(b, p):
                dve.wait_ge(nmean1_done, b + 1)
                v.tensor_tensor(dev1[:, :], meanvar1[:, 0:1], nmean1[:, :], ALU.add).then_inc(dev1_done, 1)

            def gn1_spread(b, p):
                dve.wait_ge(dev1_done, b + 1)
                if past(b, 1):
                    dve.wait_ge(gvar1_ps, b)
                v.scalar_tensor_tensor(spread1[:, :], dev1[:, :], dev1[:, :], meanvar1[:, 1:2], ALU.mult, ALU.add).then_inc(spread1_done, 1)

            def gn1_var(b, p):
                dve.wait_ge(gvar1_ps, b + 1)
                if past(b, 1):
                    dve.wait_ge(rstd1_done, b)
                v.tensor_scalar(gvar1[:, :], ps_stat[:, 0:1], GN_EPS, None, ALU.add).then_inc(gvar1_done, 1)

            def rms1(b, p):
                dve.wait_ge(ssq1_ps, b + 1)
                if past(b, 1):
                    dve.wait_ge(scale1_done, b)
                v.tensor_scalar(ssq1[:, :], ps_stat[:, 0:NT], 1.0 / C, NORM_MIN ** 2 / C, ALU.mult, ALU.max).then_inc(ssq1_done, 1)

            def k_partial_max(b, p):
                dve.wait_ge(qkv_done, NT * (b + 1))
                if past(b, 1):
                    dve.wait_ge(k_part_ps, b)
                v.tensor_reduce(k_max_part[:, :], qkv[:, :, HID:2 * HID].rearrange("p t c -> p c t"), AX.X, ALU.max).then_inc(k_part_done, 1)

            def k_maximum(b, p):
                dve.wait_ge(k_part_ps, b + 1)
                if past(b, 1):
                    dve.wait_ge(k_diag_done, b)
                v.tensor_reduce(k_max[:, :], ps_att[:, 0:128], AX.X, ALU.max).then_inc(k_max_done, 1)

            def k_diagonal(b, p):
                dve.wait_ge(k_max_done, b + 1)
                if past(b, 1):
                    dve.wait_ge(k_shift_ps, b)
                v.scalar_tensor_tensor(k_diag[:, :], ident[:, :], k_max[:, :], memk_diag[:, :], ALU.mult, ALU.max).then_inc(k_diag_done, 1)

            def k_subtract(b, p):
                dve.wait_ge(k_shift_ps, b + 1)
                if past(b, 1):
                    dve.wait_ge(context_ps, b)
                v.tensor_tensor(memk_exp[:, :], memk_t[:, :], ps_att[0:MEM, 0:HID], ALU.subtract).then_inc(memk_sub_done, 1)
                v.tensor_tensor(k_exp[:, :, :], qkv[:, :, HID:2 * HID],
                                ps_att[:, 0:HID].unsqueeze(1).to_broadcast((128, NT, HID)), ALU.subtract).then_inc(k_sub_done, 1)

            def q_maximum(b, p):
                q = qkv[:, :, 0:HID].rearrange("p t (h d) -> p t h d", h=HEADS)
                dve.wait_ge(qkv_done, NT * (b + 1))
                if past(b, 1):
                    dve.wait_ge(q_sub_done, b)
                v.tensor_reduce(q_max[:, :].rearrange("p (t h) -> p t h", h=HEADS), q, AX.X, ALU.max).then_inc(q_max_done, 1)

            def q_subtract(b, p):
                q = qkv[:, :, 0:HID].rearrange("p t (h d) -> p t h d", h=HEADS)
                dve.wait_ge(q_max_done, b + 1)
                if past(b, 1):
                    dve.wait_ge(q_t_ps, 2 * b)
                v.tensor_tensor(q_exp[:, :, :].rearrange("p (t h) d -> p t h d", h=HEADS), q,
                                q_max[:, :].rearrange("p (t h) -> p t h", h=HEADS).unsqueeze(3).to_broadcast((128, NT, HEADS, DH)),
                                ALU.subtract).then_inc(q_sub_done, 1)

            def q_sums(b, p):
                dve.wait_ge(q_exp_done, b + 1)
                if past(b, 1):
                    dve.wait_ge(q_rsum_done, b)
                v.tensor_reduce(q_sum[:, :], q_exp[:, :, :], AX.X, ALU.add).then_inc(q_sum_done, 1)

            def q_reciprocal(b, p):
                dve.wait_ge(q_sum_done, b + 1)
                if past(b, 1):
                    dve.wait_ge(q_norm_done, b)
                v.reciprocal(q_rsum[:, :], q_sum[:, :]).then_inc(q_rsum_done, 1)

            def context_sums(b, p):
                dve.wait_ge(context_ps, b + 1)
                if past(b, 1):
                    dve.wait_ge(context_done, b)
                v.reciprocal(k_rsum[:, :], ps_att[:, HID:HID + 1]).then_inc(k_rsum_done, 1)

            def context_scale(b, p):
                dve.wait_ge(k_rsum_done, b + 1)
                if past(b, 1):
                    dve.wait_ge(context_t_ps, b)
                v.scalar_tensor_tensor(context[:, :], ps_att[:, 0:HID], k_rsum[:, :], head_mask[:, :], ALU.mult, ALU.mult).then_inc(context_done, 1)

            def mix_evacuate(b, p):
                dve.wait_ge(mix_ps, b + 1)
                if past(b, 2):
                    dve.wait_ge(y_ps, b - 1)
                v.tensor_tensor(mix[p][:, :], ps_att[:, 0:C], bias_share[:, :], ALU.add).then_inc(mix_done, 1)

            def rms2_mean(b, p):
                dve.wait_ge(ssq2_sum_done, b + 1)
                if past(b, 1):
                    dve.wait_ge(scale2_done, b)
                v.tensor_scalar(ssq2[:, :], ssq2_sum[:, :], 1.0 / C, NORM_MIN ** 2 / C, ALU.mult, ALU.max).then_inc(ssq2_done, 1)

            def y_scale(b, p):
                dve.wait_ge(scale2_done, b + 1)
                if past(b, 1):
                    dve.wait_ge(y_t_ps, b)
                v.tensor_tensor(y_scaled[:, :, :], ps_y[:, :].rearrange("p (t c) -> p t c", c=C),
                                scale2[:, :].unsqueeze(2).to_broadcast((128, NT, C)), ALU.mult).then_inc(y_scaled_done, 1)

            def residual1(b, p):
                dve.wait_ge(y_t_ps, b + 1)
                dve.wait_ge(xb_loaded[p], slot_count(b, p))
                if past(b, 2):
                    dve.wait_ge(result_done, 2 * (b - 1))
                v.scalar_tensor_tensor(x2[p][:, :], ps_y[:, :], g2_c[:, :], xb[p][:, :], ALU.mult, ALU.add).then_inc(x2_done, 1)

            def gn2_stats(b, p):
                dve.wait_ge(x2_done, b + 1)
                if past(b, 1):
                    dve.wait_ge(meanvar2_done, b)
                for h in range(2):
                    last = v.bn_stats(stats2[:, h, :], x2[p][:, half(h)])
                last.then_inc(stats2_done, 1)

            def gn2_aggregate(b, p):
                if past(b, 1):
                    dve.wait_ge(gmean2_ps, b)
                    dve.wait_ge(spread2_done, b)
                dve.wait_ge(stats2_done, b + 1).then_inc(stats2_read, 1)
                v.bn_aggr(meanvar2[:, :], stats2[:, :, :].rearrange("p h s -> p (h s)")).then_inc(meanvar2_done, 1)

            def gn2_pool(b, p):
                dve.wait_ge(x2_done, b + 1)
                if past(b, 1):
                    dve.wait_ge(pooled_c_done, b)
                v.tensor_reduce(pooled[:, :].rearrange("p (i j) -> p i j", j=SP),
                                x2[p][:, :].rearrange("p (i a j b) -> p i j a b", i=SP, j=SP, b=W // SP), AX.XY, ALU.add).then_inc(pooled_done, 1)

            def gn2_mean(b, p):
                dve.wait_ge(gmean2_ps, b + 1)
                if past(b, 1):
                    dve.wait_ge(pad_hi_done, b)
                    dve.wait_ge(pad_lo_done, b)
                v.tensor_scalar(nmean2[:, :], ps_stat[:, 0:1], -1.0, None, ALU.mult).then_inc(nmean2_done, 1)

            def gn2_centre(b, p):
                dve.wait_ge(nmean2_done, b + 1)
                dve.wait_ge(pooled_done, b + 1)
                if past(b, 1):
                    dve.wait_ge(pooled_n_done, b)
                v.tensor_scalar(pooled_c[:, :], pooled[:, :], 1.0 / CELL, nmean2[:, :], ALU.mult, ALU.add).then_inc(pooled_c_done, 1)

            def gn2_deviation(b, p):
                dve.wait_ge(nmean2_done, b + 1)
                v.tensor_tensor(dev2[:, :], meanvar2[:, 0:1], nmean2[:, :], ALU.add).then_inc(dev2_done, 1)

            def gn2_spread(b, p):
                dve.wait_ge(dev2_done, b + 1)
                if past(b, 1):
                    dve.wait_ge(gvar2_ps, b)
                v.scalar_tensor_tensor(spread2[:, :], dev2[:, :], dev2[:, :], meanvar2[:, 1:2], ALU.mult, ALU.add).then_inc(spread2_done, 1)

            def gn2_var(b, p):
                dve.wait_ge(gvar2_ps, b + 1)
                if past(b, 1):
                    dve.wait_ge(rstd2_done, b)
                v.tensor_scalar(gvar2[:, :], ps_stat[:, 0:1], GN_EPS, None, ALU.add).then_inc(gvar2_done, 1)

            def image_low(b, p):
                dve.wait_ge(nmean2_done, b + 1)
                dve.wait_ge(pad_hi_done, b + 1)
                if past(b, 2):
                    dve.wait_ge(conv_ps, 2 * (b - 1))
                v.scalar_tensor_tensor(interior(pad_lo[p]), image(x2[p]), nmean2[:, :],
                                       interior(pad_hi[p]).bitcast(F32), ALU.add, ALU.subtract).then_inc(pad_lo_done, 1)

            def route_bias(b, p):
                dve.wait_ge(route_y_ps, b + 1)
                if past(b, 1):
                    dve.wait_ge(route_sum_done, b)
                v.tensor_tensor(route_y[:, :].rearrange("p (r s) -> p r s", s=SP * SP),
                                ps_stat[:, 0:RF].rearrange("p (r s) -> p r s", s=SP * SP),
                                rconv_bias[:, :].unsqueeze(2).to_broadcast((128, RC, SP * SP)), ALU.add).then_inc(route_y_done, 1)

            def route_sums(b, p):
                dve.wait_ge(route_y_done, b + 1)
                if past(b, 1):
                    dve.wait_ge(route_sum_done, b)
                    dve.wait_ge(route_z_done, b)
                for k in range(K):
                    last = v.scalar_tensor_tensor(route_terms[:, k, :], route_y[:, :], 0.0, fc[:, k, :], ALU.max, ALU.mult,
                                                  accum_out=route_sum[:, k:k + 1])
                last.then_inc(route_sum_done, 1)

            def route_logits(b, p):
                dve.wait_ge(route_sum_done, b + 1)
                if past(b, 1):
                    dve.wait_ge(route_zr_done, b)
                v.tensor_tensor(route_z[:, :], route_sum[:, :], fc_bias[:, :], ALU.add).then_inc(route_z_done, 1)

            def route_relu(b, p):
                dve.wait_ge(route_z_done, b + 1)
                if past(b, 1):
                    dve.wait_ge(route_e_done, b)
                v.tensor_scalar(route_zr[:, :], route_z[:, :], 0.0, None, ALU.max).then_inc(route_zr_done, 1)

            def gate_sum(b, p):
                dve.wait_ge(route_e_done, b + 1)
                if past(b, 1):
                    dve.wait_ge(gate_done, b)
                v.tensor_scalar(route_d[:, :], route_e[:, :], 1.0, None, ALU.add).then_inc(route_d_done, 1)

            def gate_reciprocal(b, p):
                dve.wait_ge(route_d_done, b + 1)
                if past(b, 1):
                    dve.wait_ge(gate_n_done, b)
                v.reciprocal(gate[:, :], route_d[:, :]).then_inc(gate_done, 1)

            def gate_scale(b, p):
                dve.wait_ge(gate_done, b + 1)
                dve.wait_ge(rstd2_done, b + 1)
                if past(b, 1):
                    dve.wait_ge(w_full_done, b)
                    dve.wait_ge(w_first_done, b)
                v.tensor_scalar(gate_n[:, :], gate[:, :], rstd2[:, :], None, ALU.mult).then_inc(gate_n_done, 1)

            def filters_second(b, p):
                if not past(b, 1):
                    dve.wait_ge(experts_ready, EXPERT_FILLS)
                dve.wait_ge(gate_n_done, b + 1)
                dve.wait_ge(w_first_done, b + 1)
                if past(b, 1):
                    dve.wait_ge(w_full_done, b)
                v.scalar_tensor_tensor(w_second[:, :], experts[:, 1, :], gate_n[:, 1:2], w_first[:, :], ALU.mult, ALU.add).then_inc(w_second_done, 1)

            def filters_third(b, p):
                dve.wait_ge(w_second_done, b + 1)
                if past(b, 1):
                    dve.wait_ge(w_hi_done, b)
                    dve.wait_ge(w_lo_done, b)
                v.scalar_tensor_tensor(w_full[:, :], experts[:, 2, :], gate_n[:, 2:3], w_second[:, :], ALU.mult, ALU.add).then_inc(w_full_done, 1)

            def residual2(b, p, h):
                dve.wait_ge(conv_ps, 2 * b + h + 1)
                if past(b, 2):
                    dve.wait_ge(stored[p], slot_count(b - 2, p))
                v.tensor_tensor(result[p][:, half(h)], ps_conv[h][:, :], x2[p][:, half(h)], ALU.add).then_inc(result_done, 1)

            def step(t, p):
                do(gn1_stats, t, p, 0)
                do(k_diagonal, t, p, 1)
                do(gn1_aggregate, t, p, 0)
                do(q_subtract, t, p, 1)
                do(gn1_mean, t, p, 0)
                do(k_subtract, t, p, 1)
                do(gn1_deviation, t, p, 0)
                do(gn1_spread, t, p, 0)
                do(gn1_var, t, p, 0)
                do(q_sums, t, p, 1)
                do(q_reciprocal, t, p, 1)
                do(residual1, t, p, 2)
                do(context_sums, t, p, 1)
                do(gn2_stats, t, p, 2)
                do(context_scale, t, p, 1)
                do(gn2_aggregate, t, p, 2)
                do(rms1, t, p, 0)
                do(gn2_pool, t, p, 2)
                do(gn2_mean, t, p, 2)
                do(gn2_deviation, t, p, 2)
                do(gn2_spread, t, p, 2)
                do(mix_evacuate, t, p, 1)
                do(gn2_centre, t, p, 2)
                do(gn2_var, t, p, 2)
                do(image_low, t, p, 2)
                do(route_bias, t, p, 2)
                do(route_sums, t, p, 2)
                do(rms2_mean, t, p, 1)
                do(route_logits, t, p, 2)
                do(route_relu, t, p, 2)
                do(gate_sum, t, p, 2)
                do(gate_reciprocal, t, p, 2)
                do(gate_scale, t, p, 2)
                do(residual2, t, p, 3, 0)
                do(y_scale, t, p, 1)
                do(filters_second, t, p, 2)
                do(filters_third, t, p, 2)
                do(k_partial_max, t, p, 0)
                do(q_maximum, t, p, 0)
                do(k_maximum, t, p, 0)
                do(residual2, t, p, 3, 1)

            run_steps(dve, step)

        @block.tensor
        def _(pe):
            mm = nc.tensor.matmul
            tr = nc.tensor.transpose
            pe.wait_ge(pool_consts, 1)
            pe.wait_ge(consts_loaded, CONSTS)
            for s in range(3):
                tr(ps_y[:, tile(s)], wqkv_raw[:, s, :], ident[:, :])
            tr(ps_y[:, 512:512 + RC], rconv_raw[:, :], ident[0:RC, 0:RC]).then_inc(setup_pe, 1)
            tr(ps_att[:, 0:C], wout_raw[:, :], ident[:, :])
            tr(ps_att[0:MEM, 128:256], mem_c[:, 0, :], ident[:, :])
            tr(ps_att[0:MEM, 256:384], mem_c[:, 1, :], ident[:, :]).then_inc(setup_pe, 1)
            pe.wait_ge(setup_dve, 4)

            def expert_transposes():
                pe.wait_ge(experts_loaded, 16)
                n = 0
                for k in range(K):
                    by_tap = expert_raw[:, k, :].rearrange("o (c t) -> o t c", t=TAPS)
                    for first in range(0, TAPS, 4):
                        if n >= 2:
                            pe.wait_ge(experts_ready, n - 1)
                        for tap in range(first, min(first + 4, TAPS)):
                            last = tr(ps_conv[n % 2][:, tile(tap - first)], by_tap[:, tap, :], ident[:, :])
                        last.then_inc(expert_tiles, 1)
                        n += 1

            def gn1_mean(b, p):
                pe.wait_ge(meanvar1_done, b + 1)
                if past(b, 3):
                    pe.wait_ge(route_y_done, b - 2)
                elif past(b, 1):
                    pe.wait_ge(ssq1_done, b)
                mm(ps_stat[:, 0:1], group_avg[:, :], meanvar1[:, 0:1], start=True, stop=True).then_inc(gmean1_ps, 1)

            def gn1_var(b, p):
                pe.wait_ge(spread1_done, b + 1)
                mm(ps_stat[:, 0:1], group_avg[:, :], spread1[:, :], start=True, stop=True).then_inc(gvar1_ps, 1)

            def squares1(b, p):
                pe.wait_ge(x1_sq_done, b + 1)
                pe.wait_ge(gvar1_done, b + 1)
                for t in range(NT):
                    last = mm(ps_stat[:, t:t + 1], x1_sq[:, tile(t)], ones[:, 0:1], start=True, stop=True)
                last.then_inc(ssq1_ps, 1)

            def project(b, p, t):
                if t == 0:
                    pe.wait_ge(x1_lo_done, b + 1)
                    if past(b, 1):
                        pe.wait_ge(q_t_done, 2 * b)
                if t >= 2:
                    pe.wait_ge(qkv_done, NT * b + t - 1)
                o = ps_qkv[t % 2][:, 0:QKV]
                mm(o, x1_hi[:, tile(t)], wqkv_hi[:, :], start=True, stop=False)
                mm(o, x1_hi[:, tile(t)], wqkv_lo[:, :], start=False, stop=False)
                mm(o, x1_lo[:, tile(t)], wqkv_hi[:, :], start=False, stop=True).then_inc(qkv_ps, 1)

            def k_part_transpose(b, p):
                pe.wait_ge(k_part_done, b + 1)
                if past(b, 1):
                    pe.wait_ge(mix_done, b)
                tr(ps_att[:, 0:128], k_max_part[:, :], ident[:, :]).then_inc(k_part_ps, 1)

            def k_shift(b, p):
                pe.wait_ge(k_diag_done, b + 1)
                mm(ps_att[:, 0:HID], ones_r[:, :], k_diag[:, :], start=True, stop=True).then_inc(k_shift_ps, 1)

            def contexts(b, p):
                pe.wait_ge(memk_exp_done, b + 1)
                pe.wait_ge(k_exp_done, b + 1)
                mm(ps_att[:, 0:VEXT], memk_exp[:, :], memv_t[:, :], start=True, stop=False)
                for t in range(NT):
                    last = mm(ps_att[:, 0:VEXT], k_exp[:, t, :], qkv[:, t, 2 * HID:3 * HID + 2], start=False, stop=(t == NT - 1))
                last.then_inc(context_ps, 1)

            def context_transpose(b, p):
                pe.wait_ge(context_done, b + 1)
                tr(ps_att[:, 0:HID], context[:, :], ident[:, :]).then_inc(context_t_ps, 1)

            def mixes(b, p):
                pe.wait_ge(context_t_done, b + 1)
                mm(ps_att[:, 0:C], context_t[:, :], wout_t[:, :], start=True, stop=True).then_inc(mix_ps, 1)

            def q_transpose(b, p, h):
                pe.wait_ge(q_norm_done, b + 1)
                pe.wait_ge(qkv_done, NT * (b + 1))
                for t in range(NT // 2):
                    tt = NT // 2 * h + t
                    last = tr(ps_qkv[h][:, tile(t)], q_exp[:, HEADS * tt:HEADS * (tt + 1), :].rearrange("p h d -> p (h d)"), ident[:, :])
                last.then_inc(q_t_ps, 1)

            def outputs(b, p):
                pe.wait_ge(mix_done, b + 1)
                pe.wait_ge(q_t_done, 2 * (b + 1))
                if past(b, 1):
                    pe.wait_ge(x2_done, b)
                for t in range(NT):
                    last = mm(ps_y[:, tile(t)], q_t[p][:, tile(t)], mix[p][:, :], start=True, stop=True)
                last.then_inc(y_ps, 1)

            def y_transpose(b, p):
                pe.wait_ge(y_scaled_done, b + 1)
                for t in range(NT):
                    last = tr(ps_y[:, tile(t)], y_scaled[:, t, :], ident[:, :])
                last.then_inc(y_t_ps, 1)

            def gn2_mean(b, p):
                pe.wait_ge(meanvar2_done, b + 1)
                if not (isinstance(b, int) and b + 2 >= B):
                    pe.wait_ge(ssq1_done, b + 3)
                else:
                    pe.wait_ge(route_y_done, b)
                mm(ps_stat[:, 0:1], group_avg[:, :], meanvar2[:, 0:1], start=True, stop=True).then_inc(gmean2_ps, 1)

            def gn2_var(b, p):
                pe.wait_ge(spread2_done, b + 1)
                mm(ps_stat[:, 0:1], group_avg[:, :], spread2[:, :], start=True, stop=True).then_inc(gvar2_ps, 1)

            def routing(b, p):
                pe.wait_ge(route_prod_done, b + 1)
                pe.wait_ge(gvar2_done, b + 1)
                mm(ps_stat[:, 0:RF], ones[:, :], route_prod[:, :, :].rearrange("p r s -> p (r s)"),
                   start=True, stop=True).then_inc(route_y_ps, 1)

            def convolution(b, p):
                pe.wait_ge(w_lo_done, b + 1)
                pe.wait_ge(pad_lo_done, b + 1)
                pe.wait_ge(pad_hi_done, b + 1)
                for h in range(2):
                    if past(b, 1):
                        pe.wait_ge(result_done, 2 * (b - 1) + h + 1)
                    n = 0
                    for tap in range(TAPS):
                        di, dj = tap // KW, tap % KW
                        rows, cols = slice(HH * h + di, HH * h + di + HH), slice(dj, dj + W)
                        for weight, pixels in ((w_hi[p], pad_hi[p]), (w_hi[p], pad_lo[p]), (w_lo[p], pad_hi[p])):
                            last = mm(ps_conv[h][:, :], weight[:, tap, :], pixels[:, rows, cols],
                                      start=(n == 0), stop=(n == 3 * TAPS - 1))
                            n += 1
                            if n == 3 * TAPS:
                                last.then_inc(conv_ps, 1)
                            yield

            def step(t, p):
                convolving = not isinstance(t, int) or t >= OLDEST
                products = convolution(t - OLDEST, (p - OLDEST) % 2) if convolving else iter(())

                def conv(n):
                    for _ in range(n):
                        next(products, None)

                do(y_transpose, t, p, 2)
                conv(6)
                do(gn1_mean, t, p, 0)
                do(k_shift, t, p, 1)
                conv(11)
                do(gn1_var, t, p, 0)
                conv(3)
                do(contexts, t, p, 1)
                do(squares1, t, p, 0)
                conv(1)
                do(q_transpose, t, p, 1, 0)
                do(context_transpose, t, p, 1)
                do(gn2_mean, t, p, 2)
                do(q_transpose, t, p, 1, 1)
                conv(1)
                do(mixes, t, p, 1)
                conv(2)
                do(gn2_var, t, p, 2)
                do(outputs, t, p, 1)
                conv(2)
                do(routing, t, p, 2)
                if isinstance(t, int) and t == 1:
                    expert_transposes()
                do(project, t, p, 0, 0)
                conv(4)
                do(project, t, p, 0, 1)
                conv(1)
                do(project, t, p, 0, 2)
                conv(2)
                do(project, t, p, 0, 3)
                do(project, t, p, 0, 4)
                conv(5)
                do(project, t, p, 0, 5)
                do(project, t, p, 0, 6)
                conv(2)
                do(project, t, p, 0, 7)
                conv(13)
                do(k_part_transpose, t, p, 0)
                conv(1)

            run_steps(pe, step)


_INS = ['x', 'L0_conv_g1', 'L0_conv_w_qkv', 'L0_conv_mem_kv', 'L0_conv_w_out', 'L0_conv_b_out', 'L0_conv_g2',
        'L1_conv_expert_weight', 'L1_conv_rconv_w', 'L1_conv_rconv_b', 'L1_conv_fc_w', 'L1_conv_fc_b']


def kernel(**inputs):
    import numpy as _np
    import concourse.bacc as _bacc
    from concourse import mybir as _mybir
    from concourse.bass_utils import run_bass_kernel_spmd as _run

    nc = _bacc.Bacc("TRN2", target_bir_lowering=False, num_devices=1)
    arrays, args = {}, []
    for name in _INS:
        a = _np.ascontiguousarray(inputs[name])
        arrays[f"in_{name}_dram"] = a
        args.append(nc.dram_tensor(f"in_{name}_dram", a.shape, _mybir.dt.from_np(a.dtype), kind="ExternalInput").ap())
    shape = inputs["x"].shape
    args.append(nc.dram_tensor("out_0_dram", shape, _mybir.dt.float32, kind="ExternalOutput").ap())
    attention_condconv_kernel(nc, *args)
    r = _run(nc, [arrays], core_ids=[0])
    return r.results[0]["out_0_dram"]
```

```python
from contextlib import ExitStack

import concourse.bass as bass
from concourse import mybir

F32 = mybir.dt.float32
F32R = mybir.dt.float32r
ALU = mybir.AluOpType
ACT = mybir.ActivationFunctionType
AX = mybir.AxisListType


def attention_condconv_kernel(
    nc: bass.Bass,
    x: bass.AP,
    g1: bass.AP,
    w_qkv: bass.AP,
    mem_kv: bass.AP,
    w_out: bass.AP,
    b_out: bass.AP,
    g2: bass.AP,
    expert_weight: bass.AP,
    rconv_w: bass.AP,
    rconv_b: bass.AP,
    fc_w: bass.AP,
    fc_b: bass.AP,
    out: bass.AP,
):
    B, C, H, W = x.shape
    N = H * W
    NT = N // 128
    _, HEADS, DH, MEM = mem_kv.shape
    HID = HEADS * DH
    K, CO, _, KH, KW = expert_weight.shape
    TAPS = KH * KW
    RC = rconv_w.shape[0]
    SP = 4
    CELL = (H // SP) * (W // SP)
    RF = RC * SP * SP
    GC = C // 32
    PW = W + 2
    HH = H // 2
    QKV = 3 * HID
    VEXT = HID + 2
    GN_EPS, NORM_MIN = 1e-5, 1e-12
    assert C == 128 and HID == 128 and CO == 128 and HH * W == 512 and RF <= 512 and B % 2 == 0

    x_d = x.rearrange("b c h w -> b c (h w)")
    out_d = out.rearrange("b c h w -> b c (h w)")

    ctx = ExitStack()
    with ctx:
        def sb(name, shape, dt=F32):
            return ctx.enter_context(nc.sbuf_tensor(name, shape, dt))

        def psum(name, shape):
            return ctx.enter_context(nc.psum_tensor(name, shape, F32))

        def sem(name):
            return ctx.enter_context(nc.semaphore(name))

        ident = sb("ident", [128, 128])
        ones = sb("ones", [128, 128])
        ones_r = sb("ones_r", [128, 128], F32R)
        group_avg = sb("group_avg", [128, 128])
        head_mask = sb("head_mask", [128, 128])
        minus_half = sb("minus_half", [128, NT])
        wqkv_raw = sb("wqkv_raw", [128, 3, C])
        wqkv_t = sb("wqkv_t", [128, QKV])
        wqkv_hi = sb("wqkv_hi", [128, QKV], F32R)
        wqkv_lo = sb("wqkv_lo", [128, QKV], F32R)
        wout_raw = sb("wout_raw", [128, HID])
        wout_t = sb("wout_t", [128, C])
        bias_share = sb("bias_share", [128, C])
        bias_raw = sb("bias_raw", [128, C])
        g1_c = sb("g1_c", [128, 1])
        g2_c = sb("g2_c", [128, 1])
        mem_c = sb("mem_c", [128, 2, MEM])
        memk_max = sb("memk_max", [128, 1])
        memk_diag = sb("memk_diag", [128, 128])
        memk_t = sb("memk_t", [MEM, HID])
        memv_t = sb("memv_t", [MEM, VEXT])
        expert_raw = sb("expert_raw", [128, K, C * TAPS])
        experts = sb("experts", [128, K, TAPS * CO])
        rconv_raw = sb("rconv_raw", [RC, C])
        rconv_t = sb("rconv_t", [128, RC])
        rconv_bias = sb("rconv_bias", [128, RC])
        fc = sb("fc", [128, K, RF])
        fc_bias = sb("fc_bias", [128, K])

        meanvar = sb("meanvar", [128, 2, 2])
        nmean = [sb(f"nmean{p}", [128, 2]) for p in range(2)]
        dev = sb("dev", [128, 2])
        spread = sb("spread", [128, 2])
        gvar = sb("gvar", [128, 2])
        rstd = [sb(f"rstd{p}", [128, 2]) for p in range(2)]

        xa = [sb(f"xa{p}", [128, N]) for p in range(2)]
        stats1 = sb("stats1", [128, 2, 6])
        shift1 = [sb(f"shift1_{p}", [128, 1]) for p in range(2)]
        x1 = sb("x1", [128, N])
        x1_sq = sb("x1_sq", [128, N])
        x1_hi = sb("x1_hi", [128, N], F32R)
        x1_lo = sb("x1_lo", [128, N], F32R)
        ssq1_sum = sb("ssq1_sum", [128, NT])
        ssq1 = sb("ssq1", [128, NT])
        scale1 = sb("scale1", [128, NT])
        qkv = sb("qkv", [128, NT, QKV + 2])
        k_max_part = sb("k_max_part", [128, HID])
        k_max = sb("k_max", [128, 1])
        k_diag = sb("k_diag", [128, 128], F32R)
        k_exp = sb("k_exp", [128, NT, HID])
        memk_exp = sb("memk_exp", [MEM, HID])
        q_max = sb("q_max", [128, NT * HEADS])
        q_exp = sb("q_exp", [128, NT * HEADS, DH])
        q_sum = sb("q_sum", [128, NT * HEADS])
        q_rsum = sb("q_rsum", [128, NT * HEADS])
        k_rsum = sb("k_rsum", [128, 1])
        context = sb("context", [128, HID])
        context_t = sb("context_t", [128, HID])
        q_t = [sb(f"q_t{p}", [128, N]) for p in range(2)]
        mix = [sb(f"mix{p}", [128, C]) for p in range(2)]

        xb = [sb(f"xb{p}", [128, N]) for p in range(2)]
        y_sq = sb("y_sq", [128, N])
        ssq2_sum = sb("ssq2_sum", [128, NT])
        ssq2 = sb("ssq2", [128, NT])
        scale2 = sb("scale2", [128, NT])
        y_scaled = sb("y_scaled", [128, NT, C])
        x2 = [sb(f"x2_{p}", [128, N]) for p in range(2)]
        stats2 = sb("stats2", [128, 2, 6])
        pooled = sb("pooled", [128, SP * SP])
        pooled_c = sb("pooled_c", [128, SP * SP])
        pooled_n = sb("pooled_n", [128, SP * SP])
        route_prod = sb("route_prod", [128, RC, SP * SP])
        route_y = sb("route_y", [128, RF])
        route_terms = sb("route_terms", [128, K, RF])
        route_sum = sb("route_sum", [128, K])
        route_z = sb("route_z", [128, K])
        route_zr = sb("route_zr", [128, K])
        route_e = sb("route_e", [128, K])
        route_d = sb("route_d", [128, K])
        gate = sb("gate", [128, K])
        gate_n = sb("gate_n", [128, K])
        w_first = sb("w_first", [128, TAPS * CO])
        w_second = sb("w_second", [128, TAPS * CO])
        w_full = sb("w_full", [128, TAPS * CO])
        w_hi = [sb(f"w_hi{p}", [128, TAPS, CO], F32R) for p in range(2)]
        w_lo = [sb(f"w_lo{p}", [128, TAPS, CO], F32R) for p in range(2)]
        pad_hi = [sb(f"pad_hi{p}", [128, H, PW], F32R) for p in range(2)]
        pad_lo = [sb(f"pad_lo{p}", [128, H, PW], F32R) for p in range(2)]

        result = [sb(f"result{p}", [128, N]) for p in range(2)]

        ps_conv = [psum(f"ps_conv{h}", [128, 512]) for h in range(2)]
        ps_qkv = [psum(f"ps_qkv{h}", [128, 512]) for h in range(2)]
        ps_y = psum("ps_y", [128, 1024])
        ps_att = psum("ps_att", [128, 512])
        ps_stat = psum("ps_stat", [128, 512])

        consts_loaded = sem("consts_loaded")
        late_consts_loaded = sem("late_consts_loaded")
        experts_loaded = sem("experts_loaded")
        pool_zeros = sem("pool_zeros")
        pool_consts = sem("pool_consts")
        pool_borders = sem("pool_borders")
        setup_pe = sem("setup_pe")
        setup_dve = sem("setup_dve")
        setup_act = sem("setup_act")
        expert_tiles = sem("expert_tiles")
        experts_ready = sem("experts_ready")
        xa_loaded = [sem(f"xa_loaded{p}") for p in range(2)]
        xb_loaded = [sem(f"xb_loaded{p}") for p in range(2)]
        stored = [sem(f"stored{p}") for p in range(2)]

        stats1_done = sem("stats1_done")
        meanvar1_done = sem("meanvar1_done")
        shift1_done = sem("shift1_done")
        gmean_ps = sem("gmean_ps")
        nmean_done = sem("nmean_done")
        dev_done = sem("dev_done")
        spread_done = sem("spread_done")
        gvar_ps = sem("gvar_ps")
        gvar_done = sem("gvar_done")
        rstd_done = sem("rstd_done")

        stats1_read = sem("stats1_read")
        x1_started = sem("x1_started")
        x_t_ps = sem("x_t_ps")
        ssq1_sum_done = sem("ssq1_sum_done")
        stats2_read = sem("stats2_read")
        x1_done = sem("x1_done")
        x1_hi_done = sem("x1_hi_done")
        x1_lo_done = sem("x1_lo_done")
        ssq1_done = sem("ssq1_done")
        scale1_done = sem("scale1_done")
        qkv_ps = sem("qkv_ps")
        qkv_done = sem("qkv_done")
        k_part_done = sem("k_part_done")
        k_part_ps = sem("k_part_ps")
        k_max_done = sem("k_max_done")
        k_diag_done = sem("k_diag_done")
        k_shift_ps = sem("k_shift_ps")
        k_sub_done = sem("k_sub_done")
        memk_sub_done = sem("memk_sub_done")
        k_exp_done = sem("k_exp_done")
        memk_exp_done = sem("memk_exp_done")
        q_max_done = sem("q_max_done")
        q_sub_done = sem("q_sub_done")
        q_exp_done = sem("q_exp_done")
        q_sum_done = sem("q_sum_done")
        q_rsum_done = sem("q_rsum_done")
        q_norm_done = sem("q_norm_done")
        context_ps = sem("context_ps")
        k_rsum_done = sem("k_rsum_done")
        context_done = sem("context_done")
        context_t_ps = sem("context_t_ps")
        context_t_done = sem("context_t_done")
        mix_ps = sem("mix_ps")
        mix_done = sem("mix_done")
        q_t_ps = sem("q_t_ps")
        q_t_done = sem("q_t_done")

        y_ps = sem("y_ps")
        ssq2_sum_done = sem("ssq2_sum_done")
        ssq2_done = sem("ssq2_done")
        scale2_done = sem("scale2_done")
        y_scaled_done = sem("y_scaled_done")
        y_t_ps = sem("y_t_ps")
        x2_done = sem("x2_done")
        stats2_done = sem("stats2_done")
        meanvar2_done = sem("meanvar2_done")
        pooled_done = sem("pooled_done")
        pooled_c_done = sem("pooled_c_done")
        pooled_n_done = sem("pooled_n_done")
        route_prod_done = sem("route_prod_done")
        route_y_ps = sem("route_y_ps")
        route_y_done = sem("route_y_done")
        route_sum_done = sem("route_sum_done")
        route_z_done = sem("route_z_done")
        route_zr_done = sem("route_zr_done")
        route_e_done = sem("route_e_done")
        route_d_done = sem("route_d_done")
        gate_done = sem("gate_done")
        gate_n_done = sem("gate_n_done")
        w_first_done = sem("w_first_done")
        w_second_done = sem("w_second_done")
        w_full_done = sem("w_full_done")
        w_hi_done = sem("w_hi_done")
        w_lo_done = sem("w_lo_done")
        pad_hi_done = sem("pad_hi_done")
        pad_lo_done = sem("pad_lo_done")
        conv_ps = sem("conv_ps")
        result_done = sem("result_done")

        def tile(t):
            return slice(128 * t, 128 * t + 128)

        def half(h):
            return slice(512 * h, 512 * h + 512)

        def interior(padded):
            return padded[:, :, 1:1 + W]

        def image(flat):
            return flat.rearrange("p (h w) -> p h w", w=W)

        def within(b):
            return not isinstance(b, int) or b < B

        def past(b, n):
            return not isinstance(b, int) or b >= n

        def slot_count(b, p):
            return 8 * (b - p) + 16

        OLDEST = 4
        STEPS = B + OLDEST
        FIRST, LAST = OLDEST + 2, B - 2

        def run_steps(eng, step):
            for t in range(-1, FIRST):
                step(t, t % 2)
            with eng.Fori(FIRST, LAST - 1, 2) as i:
                step(i, FIRST % 2)
                step(i + 1, 1 - FIRST % 2)
            for t in range(LAST, STEPS):
                step(t, t % 2)

        GAP = 3

        def columns(j):
            if not isinstance(j, int):
                return slice(0, 2)
            return slice(0 if j < B else 1, 2 if j >= GAP else 1)

        def turn(part, t, p, age):
            j = t - age
            if not isinstance(j, int) or 0 <= j < B + GAP:
                part(j, (p - age) % 2)

        def do(part, t, p, age, *args):
            b = t - age
            if not isinstance(b, int) or 0 <= b < B:
                part(b, (p - age) % 2, *args)

        block = ctx.enter_context(nc.Block())

        @block.sync
        def _(sp):
            def load_xa(b, p):
                if past(b, 2):
                    sp.wait_ge(x1_done, b - 1)
                    sp.wait_ge(x1_hi_done, b - 1)
                sp.dma_start(xa[p][:, :], x_d[b]).then_inc(xa_loaded[p], 16)

            def load_xb(b, p):
                if past(b, 2):
                    sp.wait_ge(x2_done, b - 1)
                sp.dma_start(xb[p][:, :], x_d[b]).then_inc(xb_loaded[p], 16)

            def store(b, p):
                sp.wait_ge(result_done, 2 * (b + 1))
                sp.dma_start(out_d[b], result[p][:, :]).then_inc(stored[p], 16)

            def load_constants():
                sp.dma_start(wqkv_raw[:, :, :], w_qkv.rearrange("(s o) c -> o s c", s=3)).then_inc(consts_loaded, 16)
                sp.dma_start(g1_c[:, :], g1.rearrange("(c a) -> c a", a=1)).then_inc(consts_loaded, 16)
                sp.dma_start(mem_c[:, :, :], mem_kv.rearrange("s h d m -> (h d) s m")).then_inc(consts_loaded, 16)
                sp.dma_start(wout_raw[:, :], w_out).then_inc(consts_loaded, 16)
                sp.dma_start(bias_raw[:, :], b_out.rearrange("(a c) -> a c", a=1).to_broadcast((128, C))).then_inc(consts_loaded, 16)
                sp.dma_start(rconv_raw[:, :], rconv_w).then_inc(consts_loaded, 16)

            def load_late_constants():
                sp.dma_start(g2_c[:, :], g2.rearrange("(c a) -> c a", a=1)).then_inc(late_consts_loaded, 16)
                sp.dma_start(rconv_bias[:, :], rconv_b.rearrange("(a r) -> a r", a=1).to_broadcast((128, RC))).then_inc(late_consts_loaded, 16)
                sp.dma_start(fc[:, :, :], fc_w.rearrange("(k c) j -> c k j", k=K)).then_inc(late_consts_loaded, 16)
                sp.dma_start(fc_bias[:, :], fc_b.rearrange("(k c) -> c k", k=K), allow_slow_non_contiguous=True).then_inc(late_consts_loaded, 16)
                sp.dma_start(expert_raw[:, :, :], expert_weight.rearrange("k o c i j -> o k (c i j)")).then_inc(experts_loaded, 16)

            def step(t, p):
                if isinstance(t, int) and t == 0:
                    load_constants()
                if isinstance(t, int) and t == 1:
                    load_late_constants()
                do(load_xa, t, p, -1)
                do(load_xb, t, p, 2)
                do(store, t, p, 4)

            run_steps(sp, step)
            for p in range(2):
                sp.wait_ge(stored[p], 16 * (B // 2))

        CONSTS, LATE_CONSTS = 16 * 6, 16 * 4
        EXPERT_FILLS = K * -(-TAPS // 4)

        @block.gpsimd
        def _(pool):
            nc.gpsimd.memset(ident[:, :], 0.0)
            nc.gpsimd.memset(group_avg[:, :], 1.0 / GC)
            nc.gpsimd.memset(head_mask[:, :], float(DH) ** -0.5)
            nc.gpsimd.memset(memv_t[:, :], 1.0)
            nc.gpsimd.memset(qkv[:, :, QKV:QKV + 2], 1.0)
            nc.gpsimd.memset(ones[:, :], 1.0).then_inc(pool_zeros, 1)
            pool.wait_ge(pool_zeros, 1)
            nc.gpsimd.affine_select(out=ident[:, :], in_=ident[:, :], compare_op=ALU.not_equal, fill=1.0,
                                    base=0, pattern=[[-1, 128]], channel_multiplier=1)
            for mask, size in ((group_avg, GC), (head_mask, DH)):
                blocks = mask[:, :].rearrange("p (g j) -> p g j", j=size)
                nc.gpsimd.affine_select(out=blocks, in_=blocks, compare_op=ALU.is_ge, fill=0.0, base=0,
                                        pattern=[[-size, 128 // size], [0, size]], channel_multiplier=1)
            nc.gpsimd.memset(minus_half[:, :], -0.5).then_inc(pool_zeros, 1)
            pool.wait_ge(pool_zeros, 2)
            for mask, size in ((group_avg, GC), (head_mask, DH)):
                blocks = mask[:, :].rearrange("p (g j) -> p g j", j=size)
                last = nc.gpsimd.affine_select(out=blocks, in_=blocks, compare_op=ALU.is_ge, fill=0.0, base=size - 1,
                                               pattern=[[size, 128 // size], [0, size]], channel_multiplier=-1)
            last.then_inc(pool_consts, 1)
            for padded in pad_hi + pad_lo:
                for column in (0, PW - 1):
                    last = nc.gpsimd.memset(padded[:, :, column:column + 1].bitcast(F32), 0.0)
            last.then_inc(pool_borders, 1)

            def inverse_deviations(j, p):
                pool.wait_ge(gvar_done, j + 1)
                if past(j, 2) and within(j - 2):
                    pool.wait_ge(x1_hi_done, j - 1)
                    pool.wait_ge(x1_done, j - 1)
                if past(j, 2 + GAP):
                    pool.wait_ge(gate_n_done, j - 1 - GAP)
                c = columns(j)
                nc.gpsimd.tensor_tensor(rstd[p][:, c], gvar[:, c], minus_half[:, c], ALU.pow).then_inc(rstd_done, 1)

            def gn1_shift(b, p):
                pool.wait_ge(rstd_done, b + 1)
                nc.gpsimd.tensor_tensor(shift1[p][:, :], nmean[p][:, 0:1], rstd[p][:, 0:1], ALU.mult).then_inc(shift1_done, 1)

            def normalise1(b, p):
                pool.wait_ge(xa_loaded[p], slot_count(b, p))
                if past(b, 1):
                    pool.wait_ge(x1_lo_done, b)
                    pool.wait_ge(x_t_ps, 2 * b)
                pool.wait_ge(shift1_done, b + 1).then_inc(x1_started, 1)
                nc.gpsimd.tensor_scalar(x1[:, :], xa[p][:, :], rstd[p][:, 0:1], shift1[p][:, :], ALU.mult, ALU.add).then_inc(x1_done, 1)

            def low1(b, p):
                pool.wait_ge(x1_done, b + 1)
                pool.wait_ge(x1_hi_done, b + 1)
                if past(b, 1):
                    pool.wait_ge(qkv_ps, NT * b)
                nc.gpsimd.tensor_tensor(x1_lo[:, :], x1[:, :], x1_hi[:, :].bitcast(F32), ALU.subtract).then_inc(x1_lo_done, 1)

            def rms1(b, p):
                pool.wait_ge(ssq1_done, b + 1)
                if past(b, 1):
                    pool.wait_ge(qkv_done, NT * b)
                nc.gpsimd.tensor_tensor(scale1[:, :], ssq1[:, :], minus_half[:, :], ALU.pow).then_inc(scale1_done, 1)

            def q_normalise(b, p):
                pool.wait_ge(q_rsum_done, b + 1)
                nc.gpsimd.tensor_tensor(q_exp[:, :, :], q_exp[:, :, :],
                                        q_rsum[:, :].unsqueeze(2).to_broadcast((128, NT * HEADS, DH)),
                                        ALU.mult).then_inc(q_norm_done, 1)

            def rms2(b, p):
                pool.wait_ge(ssq2_done, b + 1)
                if past(b, 1):
                    pool.wait_ge(y_scaled_done, b)
                nc.gpsimd.tensor_tensor(scale2[:, :], ssq2[:, :], minus_half[:, :], ALU.pow).then_inc(scale2_done, 1)

            def pooled_normalise(b, p):
                if not past(b, 1):
                    pool.wait_ge(setup_dve, 1)
                pool.wait_ge(pooled_c_done, b + 1)
                pool.wait_ge(rstd_done, b + GAP + 1)
                nc.gpsimd.tensor_tensor(pooled_n[:, :], pooled_c[:, :], rstd[(p + GAP) % 2][:, 1:2].to_broadcast((128, SP * SP)), ALU.mult).then_inc(pooled_n_done, 1)

            def routing_products(b, p):
                pool.wait_ge(pooled_n_done, b + 1)
                if past(b, 1):
                    pool.wait_ge(route_y_ps, b)
                nc.gpsimd.tensor_tensor(route_prod[:, :, :],
                                        rconv_t[:, :].unsqueeze(2).to_broadcast((128, RC, SP * SP)),
                                        pooled_n[:, :].unsqueeze(1).to_broadcast((128, RC, SP * SP)),
                                        ALU.mult).then_inc(route_prod_done, 1)

            def filters_low(b, p):
                pool.wait_ge(w_full_done, b + 1)
                pool.wait_ge(w_hi_done, b + 1)
                if past(b, 2):
                    pool.wait_ge(conv_ps, 2 * (b - 1))
                nc.gpsimd.tensor_tensor(w_lo[p][:, :, :].rearrange("p t o -> p (t o)"), w_full[:, :],
                                        w_hi[p][:, :, :].bitcast(F32).rearrange("p t o -> p (t o)"),
                                        ALU.subtract).then_inc(w_lo_done, 1)

            def step(t, p):
                turn(inverse_deviations, t, p, 1)
                do(pooled_normalise, t, p, 4)
                do(routing_products, t, p, 4)
                do(gn1_shift, t, p, 1)
                do(rms1, t, p, 2)
                do(rms2, t, p, 3)
                do(normalise1, t, p, 1)
                do(filters_low, t, p, 4)
                do(q_normalise, t, p, 2)
                do(low1, t, p, 1)

            run_steps(pool, step)

        @block.scalar
        def _(act):
            act.wait_ge(pool_zeros, 1)
            nc.scalar.activation(ones_r[:, :], ones[:, :], ACT.Copy).then_inc(setup_act, 1)
            act.wait_ge(setup_dve, 1)
            nc.scalar.activation(wqkv_hi[:, :], wqkv_t[:, :], ACT.Copy).then_inc(setup_act, 1)

            def squares1(b, p, h):
                act.wait_ge(x_t_ps, 2 * b + h + 1)
                if past(b, 1):
                    act.wait_ge(ssq1_done, b)
                    act.wait_ge(ssq1_sum_done, 2 * b)
                for t in range(NT // 2 * h, NT // 2 * (h + 1)):
                    last = nc.scalar.activation(x1_sq[:, tile(t)], ps_qkv[h][:, tile(t % (NT // 2))], ACT.Square,
                                                accum_out=ssq1_sum[:, t:t + 1])
                last.then_inc(ssq1_sum_done, 1)

            def high1(b, p):
                act.wait_ge(shift1_done, b + 1)
                act.wait_ge(xa_loaded[p], slot_count(b, p))
                if past(b, 1):
                    act.wait_ge(qkv_ps, NT * b)
                    act.wait_ge(x1_lo_done, b)
                nc.scalar.activation(x1_hi[:, :], xa[p][:, :], ACT.Identity, bias=shift1[p][:, :], scale=rstd[p][:, 0:1]).then_inc(x1_hi_done, 1)

            def qkv_evacuate(b, p, t):
                if t == 0:
                    act.wait_ge(scale1_done, b + 1)
                    if past(b, 1):
                        act.wait_ge(k_sub_done, b)
                        act.wait_ge(q_sub_done, b)
                        act.wait_ge(context_ps, b)
                act.wait_ge(qkv_ps, NT * b + t + 1)
                nc.scalar.activation(qkv[:, t, 0:QKV], ps_qkv[t % 2][:, 0:QKV], ACT.Copy, scale=scale1[:, t:t + 1]).then_inc(qkv_done, 1)

            def memk_exponent(b, p):
                act.wait_ge(memk_sub_done, b + 1)
                nc.scalar.activation(memk_exp[:, :], memk_exp[:, :], ACT.Exp).then_inc(memk_exp_done, 1)

            def k_exponent(b, p):
                act.wait_ge(k_sub_done, b + 1)
                nc.scalar.activation(k_exp[:, :, :], k_exp[:, :, :], ACT.Exp).then_inc(k_exp_done, 1)

            def q_exponent(b, p):
                act.wait_ge(q_sub_done, b + 1)
                nc.scalar.activation(q_exp[:, :, :], q_exp[:, :, :], ACT.Exp).then_inc(q_exp_done, 1)

            def context_evacuate(b, p):
                act.wait_ge(context_t_ps, b + 1)
                if past(b, 1):
                    act.wait_ge(mix_ps, b)
                nc.scalar.activation(context_t[:, :], ps_att[:, 0:HID], ACT.Copy).then_inc(context_t_done, 1)

            def q_evacuate(b, p, h):
                if past(b, 2):
                    act.wait_ge(y_ps, b - 1)
                act.wait_ge(q_t_ps, 2 * b + h + 1)
                nc.scalar.activation(q_t[p][:, half(h)], ps_qkv[h][:, :], ACT.Copy).then_inc(q_t_done, 1)

            def squares2(b, p):
                act.wait_ge(y_ps, b + 1)
                if past(b, 1):
                    act.wait_ge(ssq2_done, b)
                    act.wait_ge(ssq2_sum_done, b)
                for t in range(NT):
                    last = nc.scalar.activation(y_sq[:, tile(t)], ps_y[:, tile(t)], ACT.Square, accum_out=ssq2_sum[:, t:t + 1])
                last.then_inc(ssq2_sum_done, 1)

            def image_high(b, p):
                act.wait_ge(nmean_done, b + GAP + 1)
                if past(b, 2):
                    act.wait_ge(conv_ps, 2 * (b - 1))
                nc.scalar.activation(interior(pad_hi[p]), image(x2[p][:, :]), ACT.Identity, bias=nmean[(p + GAP) % 2][:, 1:2]).then_inc(pad_hi_done, 1)

            def gate_exponent(b, p):
                act.wait_ge(route_zr_done, b + 1)
                nc.scalar.activation(route_e[:, :], route_zr[:, :], ACT.Exp, scale=-1.0).then_inc(route_e_done, 1)

            def filters_first(b, p):
                if not past(b, 1):
                    act.wait_ge(experts_ready, EXPERT_FILLS)
                act.wait_ge(gate_n_done, b + 1)
                if past(b, 1):
                    act.wait_ge(w_second_done, b)
                nc.scalar.activation(w_first[:, :], experts[:, 0, :], ACT.Copy, scale=gate_n[:, 0:1]).then_inc(w_first_done, 1)

            def filters_high(b, p):
                act.wait_ge(w_full_done, b + 1)
                if past(b, 2):
                    act.wait_ge(conv_ps, 2 * (b - 1))
                nc.scalar.activation(w_hi[p][:, :, :].rearrange("p t o -> p (t o)"), w_full[:, :], ACT.Copy).then_inc(w_hi_done, 1)

            def experts_evacuate():
                n = 0
                for k in range(K):
                    for first in range(0, TAPS, 4):
                        taps = min(4, TAPS - first)
                        act.wait_ge(expert_tiles, n + 1)
                        last = nc.scalar.activation(experts[:, k, first * CO:(first + taps) * CO],
                                                    ps_conv[n % 2][:, 0:taps * CO], ACT.Copy).then_inc(experts_ready, 1)
                        n += 1

            def step(t, p):
                do(squares2, t, p, 3)
                do(qkv_evacuate, t, p, 2, 0)
                do(qkv_evacuate, t, p, 2, 1)
                do(gate_exponent, t, p, 4)
                do(qkv_evacuate, t, p, 2, 2)
                do(qkv_evacuate, t, p, 2, 3)
                do(filters_first, t, p, 4)
                do(qkv_evacuate, t, p, 2, 4)
                do(qkv_evacuate, t, p, 2, 5)
                do(qkv_evacuate, t, p, 2, 6)
                do(qkv_evacuate, t, p, 2, 7)
                do(filters_high, t, p, 4)
                do(q_exponent, t, p, 2)
                do(memk_exponent, t, p, 2)
                do(k_exponent, t, p, 2)
                if isinstance(t, int) and t == 2:
                    experts_evacuate()
                do(high1, t, p, 1)
                do(q_evacuate, t, p, 2, 0)
                do(context_evacuate, t, p, 2)
                do(q_evacuate, t, p, 2, 1)
                do(image_high, t, p, 3)
                do(squares1, t, p, 1, 0)
                do(squares1, t, p, 1, 1)

            run_steps(act, step)

        @block.vector
        def _(dve):
            v = nc.vector
            def constants():
                dve.wait_ge(consts_loaded, CONSTS)
                dve.wait_ge(setup_pe, 1)
                v.tensor_scalar(wqkv_t[:, :], ps_y[:, 0:QKV], g1_c[:, :], None, ALU.mult)
                v.tensor_copy(rconv_t[:, :], ps_y[:, 512:512 + RC]).then_inc(setup_dve, 1)
                dve.wait_ge(setup_act, 2)
                v.tensor_tensor(wqkv_lo[:, :], wqkv_t[:, :], wqkv_hi[:, :].bitcast(F32), ALU.subtract).then_inc(setup_dve, 1)

                dve.wait_ge(setup_pe, 2)
                v.tensor_copy(wout_t[:, :], ps_att[:, 0:C])
                v.tensor_copy(memk_t[:, :], ps_att[0:MEM, 128:256])
                v.tensor_copy(memv_t[:, 0:HID], ps_att[0:MEM, 256:384])
                v.tensor_scalar(bias_share[:, :], bias_raw[:, :], 1.0 / HEADS, None, ALU.mult)
                v.tensor_reduce(memk_max[:, :], mem_c[:, 0, :], AX.X, ALU.max).then_inc(setup_dve, 1)
                dve.wait_ge(setup_dve, 3)
                v.tensor_scalar(memk_diag[:, :], ident[:, :], memk_max[:, :], None, ALU.mult).then_inc(setup_dve, 1)
                dve.wait_ge(setup_dve, 4)

            def gn1_stats(b, p):
                dve.wait_ge(xa_loaded[p], slot_count(b, p))
                if past(b, 1):
                    dve.wait_ge(meanvar1_done, b)
                for h in range(2):
                    last = v.bn_stats(stats1[:, h, :], xa[p][:, half(h)])
                last.then_inc(stats1_done, 1)

            def gn1_aggregate(b, p):
                if past(b, 1):
                    dve.wait_ge(gmean_ps, b)
                    dve.wait_ge(spread_done, b)
                dve.wait_ge(stats1_done, b + 1).then_inc(stats1_read, 1)
                v.bn_aggr(meanvar[:, 0, :], stats1[:, :, :].rearrange("p h s -> p (h s)")).then_inc(meanvar1_done, 1)

            def means(j, p):
                dve.wait_ge(gmean_ps, j + 1)
                if past(j, 2) and within(j - 2):
                    dve.wait_ge(shift1_done, j - 1)
                if past(j, 2 + GAP):
                    dve.wait_ge(pad_hi_done, j - 1 - GAP)
                    dve.wait_ge(pad_lo_done, j - 1 - GAP)
                c = columns(j)
                v.tensor_scalar(nmean[p][:, c], ps_stat[:, c], -1.0, None, ALU.mult).then_inc(nmean_done, 1)

            def differences(j, p):
                dve.wait_ge(nmean_done, j + 1)
                c = columns(j)
                v.tensor_tensor(dev[:, c], meanvar[:, c, 0], nmean[p][:, c], ALU.add).then_inc(dev_done, 1)

            def spreads(j, p):
                dve.wait_ge(dev_done, j + 1)
                if past(j, 1):
                    dve.wait_ge(gvar_ps, j)
                c = columns(j)
                for i in range(c.start, c.stop):
                    last = v.scalar_tensor_tensor(spread[:, i:i + 1], dev[:, i:i + 1], dev[:, i:i + 1], meanvar[:, i, 1:2], ALU.mult, ALU.add)
                last.then_inc(spread_done, 1)

            def variances(j, p):
                dve.wait_ge(gvar_ps, j + 1)
                if past(j, 1):
                    dve.wait_ge(rstd_done, j)
                c = columns(j)
                v.tensor_scalar(gvar[:, c], ps_stat[:, c], GN_EPS, None, ALU.add).then_inc(gvar_done, 1)

            def rms1(b, p):
                dve.wait_ge(ssq1_sum_done, 2 * (b + 1))
                if past(b, 1):
                    dve.wait_ge(scale1_done, b)
                v.tensor_scalar(ssq1[:, :], ssq1_sum[:, :], 1.0 / C, NORM_MIN ** 2 / C, ALU.mult, ALU.max).then_inc(ssq1_done, 1)

            def k_partial_max(b, p):
                dve.wait_ge(qkv_done, NT * (b + 1))
                if past(b, 1):
                    dve.wait_ge(k_part_ps, b)
                v.tensor_reduce(k_max_part[:, :], qkv[:, :, HID:2 * HID].rearrange("p t c -> p c t"), AX.X, ALU.max).then_inc(k_part_done, 1)

            def k_maximum(b, p):
                dve.wait_ge(k_part_ps, b + 1)
                if past(b, 1):
                    dve.wait_ge(k_diag_done, b)
                v.tensor_reduce(k_max[:, :], ps_att[:, 0:128], AX.X, ALU.max).then_inc(k_max_done, 1)

            def k_diagonal(b, p):
                dve.wait_ge(k_max_done, b + 1)
                if past(b, 1):
                    dve.wait_ge(k_shift_ps, b)
                v.scalar_tensor_tensor(k_diag[:, :], ident[:, :], k_max[:, :], memk_diag[:, :], ALU.mult, ALU.max).then_inc(k_diag_done, 1)

            def k_subtract(b, p):
                dve.wait_ge(k_shift_ps, b + 1)
                if past(b, 1):
                    dve.wait_ge(context_ps, b)
                v.tensor_tensor(memk_exp[:, :], memk_t[:, :], ps_att[0:MEM, 0:HID], ALU.subtract).then_inc(memk_sub_done, 1)
                v.tensor_tensor(k_exp[:, :, :], qkv[:, :, HID:2 * HID],
                                ps_att[:, 0:HID].unsqueeze(1).to_broadcast((128, NT, HID)), ALU.subtract).then_inc(k_sub_done, 1)

            def q_maximum(b, p):
                q = qkv[:, :, 0:HID].rearrange("p t (h d) -> p t h d", h=HEADS)
                dve.wait_ge(qkv_done, NT * (b + 1))
                if past(b, 1):
                    dve.wait_ge(q_sub_done, b)
                v.tensor_reduce(q_max[:, :].rearrange("p (t h) -> p t h", h=HEADS), q, AX.X, ALU.max).then_inc(q_max_done, 1)

            def q_subtract(b, p):
                q = qkv[:, :, 0:HID].rearrange("p t (h d) -> p t h d", h=HEADS)
                dve.wait_ge(q_max_done, b + 1)
                if past(b, 1):
                    dve.wait_ge(q_t_ps, 2 * b)
                v.tensor_tensor(q_exp[:, :, :].rearrange("p (t h) d -> p t h d", h=HEADS), q,
                                q_max[:, :].rearrange("p (t h) -> p t h", h=HEADS).unsqueeze(3).to_broadcast((128, NT, HEADS, DH)),
                                ALU.subtract).then_inc(q_sub_done, 1)

            def q_sums(b, p):
                dve.wait_ge(q_exp_done, b + 1)
                if past(b, 1):
                    dve.wait_ge(q_rsum_done, b)
                v.tensor_reduce(q_sum[:, :], q_exp[:, :, :], AX.X, ALU.add).then_inc(q_sum_done, 1)

            def q_reciprocal(b, p):
                dve.wait_ge(q_sum_done, b + 1)
                if past(b, 1):
                    dve.wait_ge(q_norm_done, b)
                v.reciprocal(q_rsum[:, :], q_sum[:, :]).then_inc(q_rsum_done, 1)

            def context_sums(b, p):
                dve.wait_ge(context_ps, b + 1)
                if past(b, 1):
                    dve.wait_ge(context_done, b)
                v.reciprocal(k_rsum[:, :], ps_att[:, HID:HID + 1]).then_inc(k_rsum_done, 1)

            def context_scale(b, p):
                dve.wait_ge(k_rsum_done, b + 1)
                if past(b, 1):
                    dve.wait_ge(context_t_ps, b)
                v.scalar_tensor_tensor(context[:, :], ps_att[:, 0:HID], k_rsum[:, :], head_mask[:, :], ALU.mult, ALU.mult).then_inc(context_done, 1)

            def mix_evacuate(b, p):
                dve.wait_ge(mix_ps, b + 1)
                if past(b, 2):
                    dve.wait_ge(y_ps, b - 1)
                v.tensor_tensor(mix[p][:, :], ps_att[:, 0:C], bias_share[:, :], ALU.add).then_inc(mix_done, 1)

            def rms2_mean(b, p):
                dve.wait_ge(ssq2_sum_done, b + 1)
                if past(b, 1):
                    dve.wait_ge(scale2_done, b)
                v.tensor_scalar(ssq2[:, :], ssq2_sum[:, :], 1.0 / C, NORM_MIN ** 2 / C, ALU.mult, ALU.max).then_inc(ssq2_done, 1)

            def y_scale(b, p):
                dve.wait_ge(scale2_done, b + 1)
                if past(b, 1):
                    dve.wait_ge(y_t_ps, b)
                v.tensor_tensor(y_scaled[:, :, :], ps_y[:, :].rearrange("p (t c) -> p t c", c=C),
                                scale2[:, :].unsqueeze(2).to_broadcast((128, NT, C)), ALU.mult).then_inc(y_scaled_done, 1)

            def residual1(b, p):
                if not past(b, 1):
                    dve.wait_ge(late_consts_loaded, LATE_CONSTS)
                dve.wait_ge(y_t_ps, b + 1)
                dve.wait_ge(xb_loaded[p], slot_count(b, p))
                if past(b, 2):
                    dve.wait_ge(result_done, 2 * (b - 1))
                v.scalar_tensor_tensor(x2[p][:, :], ps_y[:, :], g2_c[:, :], xb[p][:, :], ALU.mult, ALU.add).then_inc(x2_done, 1)

            def gn2_stats(b, p):
                dve.wait_ge(x2_done, b + 1)
                if past(b, 1):
                    dve.wait_ge(meanvar2_done, b)
                for h in range(2):
                    last = v.bn_stats(stats2[:, h, :], x2[p][:, half(h)])
                last.then_inc(stats2_done, 1)

            def gn2_aggregate(b, p):
                if past(b, 1):
                    dve.wait_ge(gmean_ps, b + GAP)
                    dve.wait_ge(spread_done, b + GAP)
                dve.wait_ge(stats2_done, b + 1).then_inc(stats2_read, 1)
                v.bn_aggr(meanvar[:, 1, :], stats2[:, :, :].rearrange("p h s -> p (h s)")).then_inc(meanvar2_done, 1)

            def gn2_pool(b, p):
                dve.wait_ge(x2_done, b + 1)
                if past(b, 1):
                    dve.wait_ge(pooled_c_done, b)
                v.tensor_reduce(pooled[:, :].rearrange("p (i j) -> p i j", j=SP),
                                x2[p][:, :].rearrange("p (i a j b) -> p i j a b", i=SP, j=SP, b=W // SP), AX.XY, ALU.add).then_inc(pooled_done, 1)

            def gn2_centre(b, p):
                dve.wait_ge(nmean_done, b + GAP + 1)
                dve.wait_ge(pooled_done, b + 1)
                if past(b, 1):
                    dve.wait_ge(pooled_n_done, b)
                v.tensor_scalar(pooled_c[:, :], pooled[:, :], 1.0 / CELL, nmean[(p + GAP) % 2][:, 1:2], ALU.mult, ALU.add).then_inc(pooled_c_done, 1)

            def image_low(b, p):
                dve.wait_ge(nmean_done, b + GAP + 1)
                dve.wait_ge(pad_hi_done, b + 1)
                if past(b, 2):
                    dve.wait_ge(conv_ps, 2 * (b - 1))
                v.scalar_tensor_tensor(interior(pad_lo[p]), image(x2[p][:, :]), nmean[(p + GAP) % 2][:, 1:2],
                                       interior(pad_hi[p]).bitcast(F32), ALU.add, ALU.subtract).then_inc(pad_lo_done, 1)

            def route_bias(b, p):
                dve.wait_ge(route_y_ps, b + 1)
                if past(b, 1):
                    dve.wait_ge(route_sum_done, b)
                v.tensor_tensor(route_y[:, :].rearrange("p (r s) -> p r s", s=SP * SP),
                                ps_stat[:, 0:RF].rearrange("p (r s) -> p r s", s=SP * SP),
                                rconv_bias[:, :].unsqueeze(2).to_broadcast((128, RC, SP * SP)), ALU.add).then_inc(route_y_done, 1)

            def route_sums(b, p):
                dve.wait_ge(route_y_done, b + 1)
                if past(b, 1):
                    dve.wait_ge(route_sum_done, b)
                    dve.wait_ge(route_z_done, b)
                for k in range(K):
                    last = v.scalar_tensor_tensor(route_terms[:, k, :], route_y[:, :], 0.0, fc[:, k, :], ALU.max, ALU.mult,
                                                  accum_out=route_sum[:, k:k + 1])
                last.then_inc(route_sum_done, 1)

            def route_logits(b, p):
                dve.wait_ge(route_sum_done, b + 1)
                if past(b, 1):
                    dve.wait_ge(route_zr_done, b)
                v.tensor_tensor(route_z[:, :], route_sum[:, :], fc_bias[:, :], ALU.add).then_inc(route_z_done, 1)

            def route_relu(b, p):
                dve.wait_ge(route_z_done, b + 1)
                if past(b, 1):
                    dve.wait_ge(route_e_done, b)
                v.tensor_scalar(route_zr[:, :], route_z[:, :], 0.0, None, ALU.max).then_inc(route_zr_done, 1)

            def gate_sum(b, p):
                dve.wait_ge(route_e_done, b + 1)
                if past(b, 1):
                    dve.wait_ge(gate_done, b)
                v.tensor_scalar(route_d[:, :], route_e[:, :], 1.0, None, ALU.add).then_inc(route_d_done, 1)

            def gate_reciprocal(b, p):
                dve.wait_ge(route_d_done, b + 1)
                if past(b, 1):
                    dve.wait_ge(gate_n_done, b)
                v.reciprocal(gate[:, :], route_d[:, :]).then_inc(gate_done, 1)

            def gate_scale(b, p):
                dve.wait_ge(gate_done, b + 1)
                dve.wait_ge(rstd_done, b + GAP + 1)
                if past(b, 1):
                    dve.wait_ge(w_full_done, b)
                    dve.wait_ge(w_first_done, b)
                v.tensor_scalar(gate_n[:, :], gate[:, :], rstd[(p + GAP) % 2][:, 1:2], None, ALU.mult).then_inc(gate_n_done, 1)

            def filters_second(b, p):
                if not past(b, 1):
                    dve.wait_ge(experts_ready, EXPERT_FILLS)
                dve.wait_ge(gate_n_done, b + 1)
                dve.wait_ge(w_first_done, b + 1)
                if past(b, 1):
                    dve.wait_ge(w_full_done, b)
                v.scalar_tensor_tensor(w_second[:, :], experts[:, 1, :], gate_n[:, 1:2], w_first[:, :], ALU.mult, ALU.add).then_inc(w_second_done, 1)

            def filters_third(b, p):
                dve.wait_ge(w_second_done, b + 1)
                if past(b, 1):
                    dve.wait_ge(w_hi_done, b)
                    dve.wait_ge(w_lo_done, b)
                v.scalar_tensor_tensor(w_full[:, :], experts[:, 2, :], gate_n[:, 2:3], w_second[:, :], ALU.mult, ALU.add).then_inc(w_full_done, 1)

            def residual2(b, p, h):
                dve.wait_ge(conv_ps, 2 * b + h + 1)
                if past(b, 2):
                    dve.wait_ge(stored[p], slot_count(b - 2, p))
                v.tensor_tensor(result[p][:, half(h)], ps_conv[h][:, :], x2[p][:, half(h)], ALU.add).then_inc(result_done, 1)

            def step(t, p):
                turn(means, t, p, 0)
                turn(differences, t, p, 0)
                turn(spreads, t, p, 0)
                do(gn2_centre, t, p, 3)
                do(mix_evacuate, t, p, 2)
                turn(variances, t, p, 0)
                if isinstance(t, int) and t == 0:
                    constants()
                do(image_low, t, p, 3)
                do(rms1, t, p, 1)
                do(route_bias, t, p, 3)
                do(route_sums, t, p, 3)
                do(route_logits, t, p, 3)
                do(rms2_mean, t, p, 2)
                do(route_relu, t, p, 3)
                do(gn1_stats, t, p, -1)
                do(gate_sum, t, p, 3)
                do(gate_reciprocal, t, p, 3)
                do(gate_scale, t, p, 3)
                do(y_scale, t, p, 2)
                do(residual2, t, p, 4, 0)
                do(filters_second, t, p, 3)
                do(gn1_aggregate, t, p, -1)
                do(filters_third, t, p, 3)
                do(k_partial_max, t, p, 1)
                do(q_maximum, t, p, 1)
                do(k_maximum, t, p, 1)
                do(k_diagonal, t, p, 1)
                do(q_subtract, t, p, 1)
                do(k_subtract, t, p, 1)
                do(q_sums, t, p, 1)
                do(residual2, t, p, 4, 1)
                do(q_reciprocal, t, p, 1)
                do(residual1, t, p, 2)
                do(gn2_stats, t, p, 2)
                do(context_sums, t, p, 1)
                do(gn2_aggregate, t, p, 2)
                do(context_scale, t, p, 1)
                do(gn2_pool, t, p, 2)

            run_steps(dve, step)

        @block.tensor
        def _(pe):
            mm = nc.tensor.matmul
            tr = nc.tensor.transpose

            def constants():
                pe.wait_ge(pool_consts, 1)
                pe.wait_ge(consts_loaded, CONSTS)
                for s in range(3):
                    tr(ps_y[:, tile(s)], wqkv_raw[:, s, :], ident[:, :])
                tr(ps_y[:, 512:512 + RC], rconv_raw[:, :], ident[0:RC, 0:RC]).then_inc(setup_pe, 1)
                tr(ps_att[:, 0:C], wout_raw[:, :], ident[:, :])
                tr(ps_att[0:MEM, 128:256], mem_c[:, 0, :], ident[:, :])
                tr(ps_att[0:MEM, 256:384], mem_c[:, 1, :], ident[:, :]).then_inc(setup_pe, 1)
                pe.wait_ge(setup_dve, 4)

            def expert_transposes():
                pe.wait_ge(experts_loaded, 16)
                n = 0
                for k in range(K):
                    by_tap = expert_raw[:, k, :].rearrange("o (c t) -> o t c", t=TAPS)
                    for first in range(0, TAPS, 4):
                        if n >= 2:
                            pe.wait_ge(experts_ready, n - 1)
                        for tap in range(first, min(first + 4, TAPS)):
                            last = tr(ps_conv[n % 2][:, tile(tap - first)], by_tap[:, tap, :], ident[:, :])
                        last.then_inc(expert_tiles, 1)
                        n += 1

            def group_means(j, p):
                if not past(j, 1):
                    pe.wait_ge(pool_consts, 1)
                if within(j):
                    pe.wait_ge(meanvar1_done, j + 1)
                if past(j, GAP):
                    pe.wait_ge(meanvar2_done, j + 1 - GAP)
                if past(j, GAP + 1):
                    pe.wait_ge(route_y_done, j - GAP)
                elif past(j, 1):
                    pe.wait_ge(gvar_done, j)
                c = columns(j)
                mm(ps_stat[:, c], group_avg[:, :], meanvar[:, c, 0], start=True, stop=True).then_inc(gmean_ps, 1)

            def group_variances(j, p):
                pe.wait_ge(spread_done, j + 1)
                c = columns(j)
                mm(ps_stat[:, c], group_avg[:, :], spread[:, c], start=True, stop=True).then_inc(gvar_ps, 1)

            def x_transpose(b, p, h):
                pe.wait_ge(x1_done, b + 1)
                if past(b, 1):
                    pe.wait_ge(q_t_done, 2 * b)
                for t in range(NT // 2):
                    last = tr(ps_qkv[h][:, tile(t)], x1[:, tile(NT // 2 * h + t)], ident[:, :])
                last.then_inc(x_t_ps, 1)

            def project(b, p, t):
                if t == 0:
                    pe.wait_ge(x1_lo_done, b + 1)
                    pe.wait_ge(x1_hi_done, b + 1)
                if t < 2:
                    pe.wait_ge(ssq1_sum_done, 2 * b + t + 1)
                if t >= 2:
                    pe.wait_ge(qkv_done, NT * b + t - 1)
                o = ps_qkv[t % 2][:, 0:QKV]
                mm(o, x1_hi[:, tile(t)], wqkv_hi[:, :], start=True, stop=False)
                mm(o, x1_hi[:, tile(t)], wqkv_lo[:, :], start=False, stop=False)
                mm(o, x1_lo[:, tile(t)], wqkv_hi[:, :], start=False, stop=True).then_inc(qkv_ps, 1)

            def k_part_transpose(b, p):
                pe.wait_ge(k_part_done, b + 1)
                if past(b, 1):
                    pe.wait_ge(mix_done, b)
                tr(ps_att[:, 0:128], k_max_part[:, :], ident[:, :]).then_inc(k_part_ps, 1)

            def k_shift(b, p):
                pe.wait_ge(k_diag_done, b + 1)
                mm(ps_att[:, 0:HID], ones_r[:, :], k_diag[:, :], start=True, stop=True).then_inc(k_shift_ps, 1)

            def contexts(b, p):
                pe.wait_ge(memk_exp_done, b + 1)
                pe.wait_ge(k_exp_done, b + 1)
                mm(ps_att[:, 0:VEXT], memk_exp[:, :], memv_t[:, :], start=True, stop=False)
                for t in range(NT):
                    last = mm(ps_att[:, 0:VEXT], k_exp[:, t, :], qkv[:, t, 2 * HID:3 * HID + 2], start=False, stop=(t == NT - 1))
                last.then_inc(context_ps, 1)

            def context_transpose(b, p):
                pe.wait_ge(context_done, b + 1)
                tr(ps_att[:, 0:HID], context[:, :], ident[:, :]).then_inc(context_t_ps, 1)

            def mixes(b, p):
                pe.wait_ge(context_t_done, b + 1)
                mm(ps_att[:, 0:C], context_t[:, :], wout_t[:, :], start=True, stop=True).then_inc(mix_ps, 1)

            def q_transpose(b, p, h):
                pe.wait_ge(q_norm_done, b + 1)
                pe.wait_ge(qkv_done, NT * (b + 1))
                for t in range(NT // 2):
                    tt = NT // 2 * h + t
                    last = tr(ps_qkv[h][:, tile(t)], q_exp[:, HEADS * tt:HEADS * (tt + 1), :].rearrange("p h d -> p (h d)"), ident[:, :])
                last.then_inc(q_t_ps, 1)

            def outputs(b, p):
                pe.wait_ge(mix_done, b + 1)
                pe.wait_ge(q_t_done, 2 * (b + 1))
                if past(b, 1):
                    pe.wait_ge(x2_done, b)
                for t in range(NT):
                    last = mm(ps_y[:, tile(t)], q_t[p][:, tile(t)], mix[p][:, :], start=True, stop=True)
                last.then_inc(y_ps, 1)

            def y_transpose(b, p):
                pe.wait_ge(y_scaled_done, b + 1)
                for t in range(NT):
                    last = tr(ps_y[:, tile(t)], y_scaled[:, t, :], ident[:, :])
                last.then_inc(y_t_ps, 1)

            def routing(b, p):
                pe.wait_ge(route_prod_done, b + 1)
                pe.wait_ge(gvar_done, b + GAP + 1)
                mm(ps_stat[:, 0:RF], ones[:, :], route_prod[:, :, :].rearrange("p r s -> p (r s)"),
                   start=True, stop=True).then_inc(route_y_ps, 1)

            TAP_ORDER = [TAPS // 2] + [tap for tap in range(TAPS) if tap != TAPS // 2]

            def convolution(b, p):
                if not past(b, 1):
                    pe.wait_ge(pool_borders, 1)
                pe.wait_ge(w_lo_done, b + 1)
                pe.wait_ge(pad_lo_done, b + 1)
                pe.wait_ge(pad_hi_done, b + 1)
                for h in range(2):
                    if past(b, 1):
                        pe.wait_ge(result_done, 2 * (b - 1) + h + 1)
                    n = 0
                    for tap in TAP_ORDER:
                        down, columns_in = tap // KW - 1, slice(tap % KW, tap % KW + W)
                        top, bottom = max(HH * h, -down), min(HH * (h + 1), H - down)
                        into = ps_conv[h][:, W * (top - HH * h):W * (bottom - HH * h)]
                        for weight, pixels in ((w_hi[p], pad_hi[p]), (w_hi[p], pad_lo[p]), (w_lo[p], pad_hi[p])):
                            last = mm(into, weight[:, tap, :], pixels[:, top + down:bottom + down, columns_in],
                                      start=(n == 0), stop=(n == 3 * TAPS - 1))
                            n += 1
                            if n == 3 * TAPS:
                                last.then_inc(conv_ps, 1)
                            yield

            def step(t, p):
                convolving = not isinstance(t, int) or t >= OLDEST
                products = convolution(t - OLDEST, (p - OLDEST) % 2) if convolving else iter(())

                def conv(n):
                    for _ in range(n):
                        next(products, None)

                conv(6)
                if isinstance(t, int) and t == 2:
                    expert_transposes()
                conv(4)
                do(contexts, t, p, 2)
                conv(2)
                do(q_transpose, t, p, 2, 0)
                do(q_transpose, t, p, 2, 1)
                do(context_transpose, t, p, 2)
                turn(group_means, t, p, 0)
                conv(2)
                do(mixes, t, p, 2)
                do(x_transpose, t, p, 1, 0)
                turn(group_variances, t, p, 0)
                if isinstance(t, int) and t == 0:
                    constants()
                do(x_transpose, t, p, 1, 1)
                do(outputs, t, p, 2)
                do(routing, t, p, 3)
                conv(4)
                do(project, t, p, 1, 0)
                do(project, t, p, 1, 1)
                conv(3)
                do(project, t, p, 1, 2)
                do(project, t, p, 1, 3)
                conv(6)
                do(project, t, p, 1, 4)
                do(project, t, p, 1, 5)
                conv(3)
                do(project, t, p, 1, 6)
                do(project, t, p, 1, 7)
                conv(14)
                do(k_part_transpose, t, p, 1)
                conv(2)
                do(y_transpose, t, p, 2)
                conv(1)
                do(k_shift, t, p, 1)
                conv(7)

            run_steps(pe, step)


_INS = ['x', 'L0_conv_g1', 'L0_conv_w_qkv', 'L0_conv_mem_kv', 'L0_conv_w_out', 'L0_conv_b_out', 'L0_conv_g2',
        'L1_conv_expert_weight', 'L1_conv_rconv_w', 'L1_conv_rconv_b', 'L1_conv_fc_w', 'L1_conv_fc_b']


def kernel(**inputs):
    import numpy as _np
    import concourse.bacc as _bacc
    from concourse import mybir as _mybir
    from concourse.bass_utils import run_bass_kernel_spmd as _run

    nc = _bacc.Bacc("TRN2", target_bir_lowering=False, num_devices=1)
    arrays, args = {}, []
    for name in _INS:
        a = _np.ascontiguousarray(inputs[name])
        arrays[f"in_{name}_dram"] = a
        args.append(nc.dram_tensor(f"in_{name}_dram", a.shape, _mybir.dt.from_np(a.dtype), kind="ExternalInput").ap())
    shape = inputs["x"].shape
    args.append(nc.dram_tensor("out_0_dram", shape, _mybir.dt.float32, kind="ExternalOutput").ap())
    attention_condconv_kernel(nc, *args)
    r = _run(nc, [arrays], core_ids=[0])
    return r.results[0]["out_0_dram"]
```
